# Optimizing a Trainium2 kernel written in Bass

```python
import numpy as np
import jax
import jax.numpy as jnp

def _softmax(x, axis=-1):
    return jax.nn.softmax(x, axis=axis)
def _gelu(x):
    return jax.nn.gelu(x, approximate=True)
def _silu(x):
    return jax.nn.silu(x)
def _sigmoid(x):
    return jax.nn.sigmoid(x)
def _layernorm(x, axis=-1, eps=1e-5):
    m = jnp.mean(x, axis=axis, keepdims=True)
    v = jnp.var(x, axis=axis, keepdims=True)
    return (x - m) / jnp.sqrt(v + eps)
def _scatter_add(tgt, idx, src, axis=0):
    return tgt.at[idx].add(src)
def _segment_sum(src, seg, n):
    return jax.ops.segment_sum(src, seg, n)

kernel_name = 'mk_adj_resnorm_d2_adj_128_91160b'

def setup_inputs(seed: int = 0):
    np.random.seed(seed)
    _w = jnp.asarray
    def _rec_inputs():
        import jax
        import jax.numpy as jnp
        _gk = jax.random.key(seed)
        x = -0.000929 + 1 * jax.random.normal(jax.random.fold_in(_gk, 1), (8192, 128), jnp.float32)
        _a = jax.random.bernoulli(jax.random.fold_in(_gk, 2), 0.000976562, (8192, 8192))
        adj = _a.astype(jnp.int32)
        return x, adj
    x, adj = _rec_inputs()
    def _L0_gnn_setup():
        import jax, jax.numpy as jnp
        import numpy as np
        from jax import lax
        N = 8192
        D = 128
        CHUNK = 128
        key = jax.random.key(seed)
        k1, k2 = jax.random.split(key)
        x = jax.random.normal(k1, (N, D), dtype=jnp.float32)
        adj = jax.random.randint(k2, (N, N), 0, 2, dtype=jnp.int32)
        return {'x': x, 'adj': adj}
    _L0_gnn_all = _L0_gnn_setup()
    _L0_gnn_in = {k: v for k, v in _L0_gnn_all.items() if k in ()}
    del _L0_gnn_all

    def _L1_gnn_setup():
        import jax, jax.numpy as jnp
        import numpy as np
        N = 8192
        D_IN = 128
        D_HID = 256
        D_OUT = 128
        key = jax.random.key(seed)
        k_x, k_a, k0, k1, k2, k3 = jax.random.split(key, 6)
        x = jax.random.normal(k_x, (N, D_IN), dtype=jnp.float32)
        adj_matrix = jax.random.randint(k_a, (N, N), 0, 2, dtype=jnp.int32)
        s0 = 1.0 / np.sqrt(D_IN)
        s1 = 1.0 / np.sqrt(D_HID)
        w_self_0 = jax.random.uniform(k0, (D_HID, D_IN), jnp.float32, -s0, s0)
        w_neigh_0 = jax.random.uniform(k1, (D_HID, D_IN), jnp.float32, -s0, s0)
        w_self_1 = jax.random.uniform(k2, (D_OUT, D_HID), jnp.float32, -s1, s1)
        w_neigh_1 = jax.random.uniform(k3, (D_OUT, D_HID), jnp.float32, -s1, s1)
        return {'x': x, 'adj_matrix': adj_matrix, 'w_self_0': w_self_0, 'w_neigh_0': w_neigh_0, 'w_self_1': w_self_1, 'w_neigh_1': w_neigh_1}
    _L1_gnn_all = _L1_gnn_setup()
    _L1_gnn_in = {k: v for k, v in _L1_gnn_all.items() if k in ('w_self_0', 'w_neigh_0', 'w_self_1', 'w_neigh_1', )}
    del _L1_gnn_all

    return {
        "x": x,
        "adj": adj,
        "L1_gnn_w_self_0": _L1_gnn_in["w_self_0"],
        "L1_gnn_w_neigh_0": _L1_gnn_in["w_neigh_0"],
        "L1_gnn_w_self_1": _L1_gnn_in["w_self_1"],
        "L1_gnn_w_neigh_1": _L1_gnn_in["w_neigh_1"],
    }

def reference(x, adj, L1_gnn_w_self_0, L1_gnn_w_neigh_0, L1_gnn_w_self_1, L1_gnn_w_neigh_1):
    import jax
    import jax.numpy as jnp
    def _L0_gnn_ref(x, adj):
        import jax, jax.numpy as jnp
        import numpy as np
        from jax import lax
        N = 8192
        D = 128
        CHUNK = 128
        n, d = x.shape
        neg = jnp.finfo(x.dtype).min
        adj_chunks = adj.reshape(n // CHUNK, CHUNK, n)

        def step(carry, a):
            mask = a != 0
            masked = jnp.where(mask[:, :, None], x[None, :, :], neg)
            m = jnp.max(masked, axis=1)
            has_nbr = jnp.any(mask, axis=1)
            out = jnp.where(has_nbr[:, None], m, jnp.zeros((), x.dtype))
            return (carry, out)
        _, out = lax.scan(step, None, adj_chunks)
        return out.reshape(n, d)

    def _L1_gnn_ref(x, adj_matrix, w_self_0, w_neigh_0, w_self_1, w_neigh_1):
        import jax, jax.numpy as jnp
        import numpy as np
        N = 8192
        D_IN = 128
        D_HID = 256
        D_OUT = 128
        A = adj_matrix.astype(x.dtype)

        def layer(h, w_self, w_neigh):
            neigh = A @ h
            return jax.nn.relu(h @ w_self.T + neigh @ w_neigh.T)
        h = layer(x, w_self_0, w_neigh_0)
        return layer(h, w_self_1, w_neigh_1)

    x = _layernorm(x + _L0_gnn_ref(x, adj), axis=-1)
    x = _layernorm(x + _L1_gnn_ref(x, adj, L1_gnn_w_self_0, L1_gnn_w_neigh_0, L1_gnn_w_self_1, L1_gnn_w_neigh_1), axis=-1)
    return x


_drawn_inputs = setup_inputs


def setup_inputs(seed=0):
    import zlib

    import numpy as np

    out = dict(_drawn_inputs(seed))
    spreads = {}
    factors = {}
    for name, (base, spread) in spreads.items():
        noise = np.random.default_rng([zlib.crc32(name.encode()), seed]).standard_normal(out[name].shape)
        drawn = base * np.exp(spread * noise) if base else spread * noise
        out[name] = jnp.asarray(drawn.astype(out[name].dtype))
    for name, factor in factors.items():
        out[name] = (out[name] * factor).astype(out[name].dtype)
    return out
```

```python
import concourse.bass as bass
from concourse import mybir
from contextlib import ExitStack


def graph_max_then_sum_layers(nc, x, adj, w_self_0, w_neigh_0, w_self_1, w_neigh_1, out):
    fp32 = mybir.dt.float32
    bf16 = mybir.dt.bfloat16
    fp16 = mybir.dt.float16
    fp8 = mybir.dt.float8e4
    i32 = mybir.dt.int32
    u32 = mybir.dt.uint32
    u16 = mybir.dt.uint16
    ALU = mybir.AluOpType
    ACT = mybir.ActivationFunctionType
    AX = mybir.AxisListType

    N, D = x.shape
    P = 128
    H = w_self_0.shape[0]
    HK = H // P
    NT = N // P
    ST = 8
    NG = NT // ST
    GR = ST * P
    WB = 16
    NW = N // WB
    WT = P // WB
    TOP = 24
    LEVELS = 3
    LC = 32
    C_DEG, C_ROW = 24, 25
    CAPS = [24, 12, 11, 10, 9, 8, 7, 6]
    G_AT = [0, 24, 0, 12, 24, 0, 12, 24]
    EPS = 1e-5
    FP8_ONE = 9
    DEG_BIAS = -7.0 / 16.0
    DEG_BASE = N * DEG_BIAS * DEG_BIAS
    X_SCALE = 4096.0
    NEGATIVE = -3.4028234663852886e38
    DEG_PARTS = 8
    DP = N // DEG_PARTS

    list_dram = nc.dram_tensor("neighbour_lists", (N, LC), u32, kind="Internal").ap()
    max_dram = nc.dram_tensor("neighbour_max", (N, D), fp32, kind="Internal").ap()
    x1_dram = nc.dram_tensor("layer0_out", (N, D), fp32, kind="Internal").ap()

    def group_rows(t, u):
        return t[bass.ds(u * GR, GR), :].rearrange("(s p) d -> p s d", p=P)

    class Chain:

        def __init__(self, eng, sem):
            self.eng, self.sem, self.n = eng, sem, 0

        def __call__(self, ins):
            ins.then_inc(self.sem, 1)
            self.n += 1
            return self.n

        def wait(self, n=None):
            if self.n:
                self.eng.wait_ge(self.sem, self.n if n is None else n)

        def restart(self):
            if self.n:
                self.wait()
                self.eng.sem_clear(self.sem)
            self.n = 0

    def after(eng, sem, value, first):
        if not isinstance(value, int) or value > 0:
            eng.wait_ge(sem, value)

    with ExitStack() as whole:
        def allocator(stack):
            def sb(name, shape, dt):
                return stack.enter_context(nc.sbuf_tensor("sb_" + name, shape, dt))

            def pb(name, shape, dt):
                return stack.enter_context(nc.psum_tensor("ps_" + name, shape, dt))

            def sem(name):
                return stack.enter_context(nc.semaphore(name))
            return sb, pb, sem

        sb, pb, sem = allocator(whole)
        adj_t_bits = sb("adj_t_bits", [P, NT, NW], u16)
        feat_hi = sb("feat_hi", [P, NT, D], fp16)
        feat_lo = sb("feat_lo", [P, NT, D], fp16)
        ident = sb("ident", [P, P], fp32)
        flag = sb("flag", [P, 1], fp32)
        flag_all = sb("flag_all", [P, 1], fp32)
        flag_word = sb("flag_word", [P, 1], i32)

        waits = {e: sem(f"waits_{n}") for n, e in enumerate((nc.tensor.engine, nc.scalar.engine, nc.gpsimd.engine, nc.vector.engine, nc.sync.engine))}

        def stand_apart(eng):
            eng.sem_inc(waits[eng.engine], 1)

        with ExitStack() as stage:
            sb, pb, sem = allocator(stage)
            adj_rows = [sb(f"adj_rows{i}", [P, N], i32) for i in range(2)]
            gathered = sb("gathered", [P, 36, D], fp32)
            ones = sb("ones", [P, P], fp32)
            pow2 = sb("pow2", [P, WB], fp32)
            row_pack = sb("row_pack", [P, WB, P], bf16)
            col_terms = sb("col_terms", [P, WT, WB], fp32)
            col_sum = sb("col_sum", [P, WT], fp32)
            col_pack = sb("col_pack", [P, WT], bf16)
            deg_bias = sb("deg_bias", [P, 1], fp32)
            eps = sb("eps", [P, 1], fp32)
            caps = sb("caps", [P, ST], fp32)
            local_row = sb("local_row", [P, ST], i32)
            local_rowf = sb("local_rowf", [P, ST], fp32)
            global_row = sb("global_row", [P, ST], fp32)
            rest = sb("rest", [P, NW], fp32)
            word = sb("word", [P, ST, TOP], fp32)
            word_at = sb("word_at", [P, ST, TOP], u32)
            base = sb("base", [P, ST, TOP], fp32)
            bit = sb("bit", [P, ST, LEVELS, TOP], fp32)
            cand = sb("cand", [P, ST, LEVELS, TOP], fp32)
            near = sb("near", [P, ST, TOP], fp32)
            near_on = sb("near_on", [P, ST, TOP], fp32)
            deg_parts = sb("deg_parts", [P, ST, DEG_PARTS], fp32)
            deg = sb("deg", [P, ST], fp32)
            listed = sb("listed", [P, ST], fp32)
            key = sb("key", [P, ST], fp32)
            key_diag = sb("key_diag", [P, ST // 2, P], fp32)
            rank_junk = sb("rank_junk", [P, GR], mybir.dt.uint8)
            rank = sb("rank", [P, ST], fp32)
            rank_u = sb("rank_u", [P, ST], u32)
            record = sb("record", [P, ST, LC], u32)
            lists = sb("lists", [P, ST, LC], u32)
            has_near = sb("has_near", [P, ST], fp32)
            over = sb("over", [P, ST], fp32)
            over1 = sb("over1", [P, 1], fp32)
            near_max = [sb(f"near_max{i}", [P, D], fp32) for i in range(2)]
            x_nat = [f[:, NT - ST:NT, :].bitcast(fp32).rearrange("p s (h d) -> p (s h d)", h=1).rearrange("p (s d) -> p s d", d=D)
                     for f in (feat_hi, feat_lo)]
            m_nat = sb("m_nat", [P, ST, D], fp32)
            stats = sb("stats", [P, ST, 6], fp32)
            moments = sb("moments", [P, ST, 2], fp32)
            std = sb("std", [P, ST], fp32)
            rstd = sb("rstd", [P, ST], fp32)
            pw = [pb(f"words{i}", [P, NW], fp32) for i in range(2)]
            pt = [pb(f"words_t{i}", [P, NT * WT], fp32) for i in range(2)]
            pk = [pb(f"keys{i}", [P, GR // 2], fp32) for i in range(2)]

            deg_junk = [sb(f"deg_junk{i}", [P, DP], fp8) for i in range(2)]

            adj_landed = [sem(f"adj_landed{i}") for i in range(2)]
            const_a = sem("const_a")
            const_v = sem("const_v")
            words_ready = sem("words_ready")
            words_read = sem("words_read")
            words_t_ready = sem("words_t_ready")
            words_t_read = sem("words_t_read")
            deg_ready = sem("deg_ready")
            deg_read = sem("deg_read")
            diag_ready = sem("diag_ready")
            keys_ready = sem("keys_ready")
            keys_read = sem("keys_read")
            vec = sem("vec")
            act_own = sem("act_own")
            pool_own = sem("pool_own")
            records_ready = sem("records_ready")
            records_stored = sem("records_stored")
            lists_landed = sem("lists_landed")
            gather_landed = [sem(f"gather_landed{s}") for s in range(ST)]
            max_ready = sem("max_ready")
            max_stored = [sem(f"max_stored{i}") for i in range(2)]
            nat_landed = sem("nat_landed")
            var_ready = sem("var_ready")
            std_ready = sem("std_ready")
            x1_ready = sem("x1_ready")
            x1_stored = sem("x1_stored")
            block = stage.enter_context(nc.Block())

            @block.sync
            def _(sync):
                def group(u):
                    for t in range(ST):
                        after(sync, words_t_ready, u * ST + t - 1, u)
                        after(sync, deg_ready, u * ST + t - 1, u)
                        sync.dma_start(adj_rows[t % 2][:, :], adj[bass.ds((u * ST + t) * P, P), :]).then_inc(adj_landed[t % 2], 16)
                group(0)
                if NG > 1:
                    with sync.Fori(1, NG) as u:
                        group(u)

            @block.tensor
            def _(pe):
                pe.wait_ge(const_v, 1)

                def group(u):
                    for t in range(ST):
                        by_byte = adj_rows[t % 2][:, :].bitcast(fp8)
                        by_word = by_byte.rearrange("p (c k b) -> p c k b", k=WB, b=4)
                        by_block = by_byte.rearrange("p (j q b) -> p j q b", q=P, b=4)
                        pe.wait_ge(adj_landed[t % 2], (u * (ST // 2) + t // 2 + 1) * 16)
                        after(pe, words_read, u * ST + t - 1, u)
                        stand_apart(pe)
                        for k in range(WB):
                            last = nc.tensor.matmul(pw[t % 2][:, :], row_pack[:, k, :], by_word[:, :, k, 0], start=(k == 0), stop=(k == WB - 1))
                        last.then_inc(words_ready, 1)
                        after(pe, words_t_read, u * ST + t - 1, u)
                        stand_apart(pe)
                        for j in range(NT):
                            last = nc.tensor.matmul(pt[t % 2][:, j * WT:(j + 1) * WT], by_block[:, j, :, 0], col_pack[:, :], start=True, stop=True)
                        last.then_inc(words_t_ready, 1)
                    for half in range(2):
                        pe.wait_ge(diag_ready, u * 2 + half + 1)
                        nc.tensor.matmul(pk[half][:, :], ones[:, :], key_diag[:, :, :].rearrange("p s q -> p (s q)"), start=True, stop=True).then_inc(keys_ready, 1)
                group(0)
                if NG > 1:
                    with pe.Fori(1, NG) as u:
                        group(u)

            @block.scalar
            def _(act):
                a = Chain(act, act_own)
                act.wait_ge(const_a, 1)

                def root(norm):
                    act.wait_ge(var_ready, norm + 1)
                    nc.scalar.activation(std[:, :], moments[:, :, 1], ACT.Sqrt, bias=eps[:, :]).then_inc(std_ready, 1)

                def group(u, norm):
                    if True:
                        for t in range(ST):
                            act.wait_ge(adj_landed[t % 2], (u * (ST // 2) + t // 2 + 1) * 16)
                            if t == 0:
                                after(act, deg_read, u, u)
                            stand_apart(act)
                            for c in range(DEG_PARTS):
                                if a.n >= 2:
                                    a.wait(a.n - 1)
                                a(nc.scalar.activation(deg_junk[c % 2][:, :], adj_rows[t % 2][:, c * DP:(c + 1) * DP], ACT.Square,
                                                       bias=deg_bias[:, :], accum_out=deg_parts[:, t, c:c + 1], saturate=False))
                            a.wait()
                            act.sem_inc(deg_ready, 1)
                            act.wait_ge(words_t_ready, u * ST + t + 1)
                            nc.scalar.activation(adj_t_bits[:, :, bass.ds((u * ST + t) * WT, WT)],
                                                 pt[t % 2][:, :].rearrange("p (j w) -> p j w", w=WT), ACT.Copy).then_inc(words_t_read, 1)
                            if t == 1 and norm is not None:
                                root(norm)
                    a.restart()
                group(0, None)
                group(1, None)
                if NG > 2:
                    with act.Fori(2, NG) as u:
                        group(u, u - 2)
                root(NG - 2)
                root(NG - 1)

            @block.gpsimd
            def _(pool):
                pool.memset(ident[:, :], 0.0).then_inc(pool_own, 1)
                pool.wait_ge(pool_own, 1)
                pool.affine_select(out=ident[:, :], in_=ident[:, :], compare_op=ALU.not_equal, fill=1.0, base=0,
                                   pattern=[[-1, P]], channel_multiplier=1).then_inc(pool_own, 1)
                pool.memset(ones[:, :], 1.0).then_inc(pool_own, 1)
                for k in range(WB):
                    pool.memset(pow2[:, k:k + 1], 2.0 ** (k + FP8_ONE)).then_inc(pool_own, 1)
                for s in range(ST):
                    pool.memset(caps[:, s:s + 1], float(CAPS[s])).then_inc(pool_own, 1)
                pool.memset(deg_bias[:, :], DEG_BIAS).then_inc(pool_own, 1)
                pool.memset(eps[:, :], EPS).then_inc(pool_own, 1)
                pool.iota(local_row[:, :], [[P, ST]], channel_multiplier=1).then_inc(pool_own, 1)
                pool.memset(flag[:, :], 0.0).then_inc(pool_own, 1)
                done = 2 + 1 + WB + ST + 4
                pool.wait_ge(pool_own, done)
                pool.sem_inc(const_a, 1)

                def store_lists(u):
                    pool.wait_ge(records_ready, u + 1)
                    stand_apart(pool)
                    for t in range(ST):
                        pool.indirect_dma_start(list_dram, bass.IndirectOffsetOnAxis(ap=rank_u[:, t:t + 1], axis=0),
                                                record[:, t, :], None, bounds_check=N - 1, oob_is_err=False).then_inc(records_stored, 16)

                def load_natural(u):
                    for par in range(2):
                        pool.wait_ge(max_stored[par], (u + 1) * (ST // 2) * 16)
                        stand_apart(pool)
                    after(pool, x1_stored, u * 16, u)
                    stand_apart(pool)
                    pool.dma_start(m_nat[:, :, :], group_rows(max_dram, u)).then_inc(nat_landed, 16)
                    for half in range(2):
                        pool.dma_start(x_nat[half], group_rows(x, u)[:, half * ST // 2:(half + 1) * ST // 2, :]).then_inc(nat_landed, 16)

                def store_x1(u):
                    pool.wait_ge(x1_ready, u + 1)
                    stand_apart(pool)
                    pool.dma_start(group_rows(x1_dram, u), m_nat[:, :, :]).then_inc(x1_stored, 16)

                def store_max(u, s):
                    pool.wait_ge(max_ready, u * ST + s + 1)
                    stand_apart(pool)
                    pool.indirect_dma_start(max_dram, bass.IndirectOffsetOnAxis(ap=lists[:, s, C_ROW:C_ROW + 1], axis=0),
                                            near_max[s % 2][:, :], None, bounds_check=N - 1, oob_is_err=False).then_inc(max_stored[s % 2], 16)

                def gather(u):
                    pool.wait_ge(records_stored, (u + 1) * ST * 16)
                    stand_apart(pool)
                    pool.dma_start(lists[:, :, :], group_rows(list_dram, u)).then_inc(lists_landed, 16)
                    pool.wait_ge(lists_landed, (u + 1) * 16)
                    stand_apart(pool)
                    for s in range(ST):
                        if s >= 2:
                            pool.wait_ge(max_ready, u * ST + s - 1)
                            stand_apart(pool)
                        for k in range(CAPS[s]):
                            pool.indirect_dma_start(gathered[:, G_AT[s] + k, :], None, x,
                                                    bass.IndirectOffsetOnAxis(ap=lists[:, s, k:k + 1], axis=0),
                                                    bounds_check=N - 1, oob_is_err=False).then_inc(gather_landed[s], 16)
                        if s >= 1:
                            store_max(u, s - 1)
                    store_max(u, ST - 1)

                store_lists(0)
                gather(0)
                store_lists(1)
                load_natural(0)
                gather(1)
                if NG > 2:
                    with pool.Fori(2, NG) as u:
                        store_lists(u)
                        store_x1(u - 2)
                        load_natural(u - 1)
                        gather(u)
                store_x1(NG - 2)
                load_natural(NG - 1)
                store_x1(NG - 1)
                pool.wait_ge(x1_stored, NG * 16)
                stand_apart(pool)

            @block.vector
            def _(dve):
                v = Chain(dve, vec)
                TT, TS, STT = nc.vector.tensor_tensor, nc.vector.tensor_scalar, nc.vector.scalar_tensor_tensor
                dve.wait_ge(const_a, 1)
                v(TT(row_pack[:, :, :], ident[:, :].unsqueeze(1).to_broadcast([P, WB, P]),
                     pow2[:, :].unsqueeze(2).to_broadcast([P, WB, P]), ALU.mult))
                v(TT(col_terms[:, :, :], ident[:, :].rearrange("p (m k) -> p m k", k=WB),
                     pow2[:, :].unsqueeze(1).to_broadcast([P, WT, WB]), ALU.mult))
                v(nc.vector.tensor_copy(local_rowf[:, :], local_row[:, :]))
                v(nc.vector.tensor_copy(global_row[:, :], local_row[:, :]))
                v(nc.vector.memset(record[:, :, :].bitcast(fp32), 0.0))
                v.wait()
                v(nc.vector.tensor_reduce(col_sum[:, :], col_terms[:, :, :], AX.X, ALU.add))
                v.wait()
                v(nc.vector.tensor_copy(col_pack[:, :], col_sum[:, :]))
                v.wait()
                dve.sem_inc(const_v, 1)

                def extract(u, t):
                    dve.wait_ge(words_ready, u * ST + t + 1)
                    stand_apart(dve)
                    source = pw[t % 2][:, :]
                    for r in range(TOP // 8):
                        eight = word[:, t, 8 * r:8 * r + 8]
                        v(nc.vector.max(eight, source))
                        v.wait()
                        v(nc.vector.max_index(word_at[:, t, 8 * r:8 * r + 8], eight, source))
                        if r < TOP // 8 - 1:
                            v(nc.vector.match_replace(rest[:, :], eight, source, 0.0))
                            source = rest[:, :]
                            if r == 0:
                                v.wait()
                                dve.sem_inc(words_read, 1)
                        v.wait()

                def neighbours(u):
                    b = [bit[:, :, lv, :] for lv in range(LEVELS)]
                    left = word[:, :, :]
                    v(TS(base[:, :, :], word_at[:, :, :], float(WB), float(1 - 127), ALU.mult, ALU.add))
                    for lv in range(LEVELS):
                        v(TS(b[lv].bitcast(u32), left.bitcast(u32), 0x7F800000, None, ALU.bitwise_and))
                        v.wait()
                        if lv < LEVELS - 1:
                            v(TT(left, left, b[lv], ALU.subtract))
                            v.wait()
                    v(TS(cand[:, :, :, :].bitcast(u32), bit[:, :, :, :].bitcast(u32), 23, None, ALU.logical_shift_right))
                    v.wait()
                    v(TT(cand[:, :, :, :], cand[:, :, :, :].bitcast(u32), base[:, :, :].unsqueeze(2).to_broadcast([P, ST, LEVELS, TOP]), ALU.add))
                    v.wait()
                    v(STT(cand[:, :, :, :], bit[:, :, :, :], 0.0, cand[:, :, :, :], ALU.is_gt, ALU.mult))
                    v.wait()
                    for r in range(TOP // 8):
                        for t in range(ST):
                            v(nc.vector.max(near[:, t, 8 * r:8 * r + 8], cand[:, t, :, :].rearrange("p l k -> p (l k)")))
                        v.wait()
                        if r < TOP // 8 - 1:
                            for t in range(ST):
                                flat = cand[:, t, :, :].rearrange("p l k -> p (l k)")
                                v(nc.vector.match_replace(flat, near[:, t, 8 * r:8 * r + 8], flat, 0.0))
                            v.wait()
                    dve.wait_ge(deg_ready, (u + 1) * ST)
                    v(nc.vector.tensor_reduce(deg[:, :], deg_parts[:, :, :], AX.X, ALU.add))
                    v(TS(near_on[:, :, :], near[:, :, :], 0.0, None, ALU.is_gt))
                    v.wait()
                    dve.sem_inc(deg_read, 1)
                    v(TS(deg[:, :], deg[:, :], -DEG_BASE, 8.0, ALU.add, ALU.mult))
                    v(nc.vector.tensor_reduce(listed[:, :], near_on[:, :, :], AX.X, ALU.add))
                    v.wait()
                    v(TT(over[:, :], deg[:, :], listed[:, :], ALU.not_equal))
                    v(TS(key[:, :], deg[:, :], 64.0, float(GR), ALU.min, ALU.mult))
                    v.wait()
                    v(nc.vector.tensor_reduce(over1[:, :], over[:, :], AX.X, ALU.max))
                    v(TT(key[:, :], key[:, :], local_rowf[:, :], ALU.add))
                    v.wait()
                    v(TT(flag[:, :], flag[:, :], over1[:, :], ALU.max))

                def sort_rows(u):
                    for half in range(2):
                        if half:
                            dve.wait_ge(keys_ready, u * 2 + 1)
                        n = ST // 2
                        v(TT(key_diag[:, :, :], ident[:, :].unsqueeze(1).to_broadcast([P, n, P]),
                             key[:, half * n:half * n + n].unsqueeze(2).to_broadcast([P, n, P]), ALU.mult))
                        v.wait()
                        dve.sem_inc(diag_ready, 1)
                    v(TS(near_on[:, :, :], near_on[:, :, :], -1.0, 1.0, ALU.mult, ALU.add))
                    v.wait()
                    v(TT(near_on[:, :, :], near_on[:, :, :], near[:, :, 0:1].to_broadcast([P, ST, TOP]), ALU.mult))
                    v.wait()
                    v(TT(near[:, :, :], near[:, :, :], near_on[:, :, :], ALU.add))
                    after(dve, records_stored, u * ST * 16, u)
                    v.wait()
                    v(TS(near[:, :, :], near[:, :, :], 1.0, float(N), ALU.max, ALU.min))
                    v.wait()
                    v(TS(record[:, :, 0:TOP], near[:, :, :], -1.0, None, ALU.add))
                    v(TS(record[:, :, C_DEG], deg[:, :], 64.0, None, ALU.min))
                    v(nc.vector.tensor_copy(record[:, :, C_ROW], global_row[:, :]))
                    for half in range(2):
                        dve.wait_ge(keys_ready, u * 2 + half + 1)
                    for t in range(ST):
                        for half in range(2):
                            v(TS(rank_junk[:, half * GR // 2:(half + 1) * GR // 2], pk[half][:, :], key[:, t:t + 1],
                                 0.0 if half == 0 else rank[:, t:t + 1], ALU.is_gt, ALU.add, accum_out=rank[:, t:t + 1]))
                            if half == 0:
                                v.wait()
                    v.wait()
                    v(TT(rank[:, :], rank[:, :], global_row[:, :], ALU.add))
                    v.wait()
                    v(TT(rank_u[:, :], rank[:, :], local_rowf[:, :], ALU.subtract))
                    v.wait()
                    v(TS(global_row[:, :], global_row[:, :], float(GR), None, ALU.add))
                    dve.sem_inc(records_ready, 1)

                def reduce_max(u, s):
                    dve.wait_ge(gather_landed[s], (u + 1) * CAPS[s] * 16)
                    if s == 0:
                        v(TS(has_near[:, :], lists[:, :, C_DEG], 0.0, None, ALU.is_gt))
                        v(TT(over[:, :], lists[:, :, C_DEG], caps[:, :], ALU.is_gt))
                        v.wait()
                        v(nc.vector.tensor_reduce(over1[:, :], over[:, :], AX.X, ALU.max))
                        v.wait()
                        v(TT(flag[:, :], flag[:, :], over1[:, :], ALU.max))
                    after(dve, max_stored[s % 2], (u * (ST // 2) + s // 2) * 16, u)
                    v(nc.vector.tensor_reduce(near_max[s % 2][:, :], gathered[:, G_AT[s]:G_AT[s] + CAPS[s], :].rearrange("p k d -> p d k"), AX.X, ALU.max))
                    v.wait()
                    v(TS(near_max[s % 2][:, :], near_max[s % 2][:, :], has_near[:, s:s + 1], None, ALU.mult))
                    v.wait()
                    dve.sem_inc(max_ready, 1)

                def normalise(u):
                    dve.wait_ge(nat_landed, (u + 1) * 48)
                    for half in range(2):
                        part = m_nat[:, half * ST // 2:(half + 1) * ST // 2, :]
                        v(TT(part, part, x_nat[half], ALU.add))
                    v.wait()
                    for s in range(ST):
                        v(nc.vector.bn_stats(stats[:, s, :], m_nat[:, s, :]))
                    v.wait()
                    for s in range(ST):
                        v(nc.vector.bn_aggr(moments[:, s, :], stats[:, s, :]))
                    v.wait()
                    dve.sem_inc(var_ready, 1)
                    dve.wait_ge(std_ready, u + 1)
                    v(nc.vector.reciprocal(rstd[:, :], std[:, :]))
                    v.wait()
                    for s in range(ST):
                        v(TS(m_nat[:, s, :], m_nat[:, s, :], moments[:, s, 0:1], rstd[:, s:s + 1], ALU.subtract, ALU.mult))
                    v.wait()
                    dve.sem_inc(x1_ready, 1)
                    hi = feat_hi[:, bass.ds(u * ST, ST), :]
                    v(TS(hi, m_nat[:, :, :], X_SCALE, None, ALU.mult))
                    v.wait()
                    v(STT(feat_lo[:, bass.ds(u * ST, ST), :], m_nat[:, :, :], X_SCALE, hi, ALU.mult, ALU.subtract))

                def group(u, reduced, normed):
                    for t in range(ST):
                        if u is not None:
                            extract(u, t)
                        if t == 1 and normed is not None:
                            normalise(normed)
                        if reduced is not None and t >= 2:
                            reduce_max(reduced, t - 2)
                    if u is not None:
                        neighbours(u)
                        sort_rows(u)
                    if reduced is not None:
                        reduce_max(reduced, ST - 2)
                        reduce_max(reduced, ST - 1)
                    v.restart()

                v.restart()
                group(0, None, None)
                group(1, 0, None)
                if NG > 2:
                    with dve.Fori(2, NG) as u:
                        group(u, u - 1, u - 2)
                group(None, NG - 1, NG - 2)
                group(None, None, NG - 1)

        flag_reduced = sem("flag_reduced")
        flag_own = sem("flag_own")
        with nc.Block() as block:
            @block.gpsimd
            def _(pool):
                pool.partition_all_reduce(flag_all[:, :], flag[:, :], P, bass.bass_isa.ReduceOp.max).then_inc(flag_reduced, 1)

            @block.vector
            def _(dve):
                dve.wait_ge(flag_reduced, 1)
                nc.vector.tensor_scalar(flag_all[:, :], flag_all[:, :], 0.0, None, ALU.is_gt).then_inc(flag_own, 1)
                dve.wait_ge(flag_own, 1)
                nc.vector.tensor_copy(flag_word[:, :], flag_all[:, :]).then_inc(flag_own, 1)
                dve.wait_ge(flag_own, 2)

        def general(eng):
            return eng.value_load(flag_word[0:1, 0:1], min_val=0, max_val=1)

        with ExitStack() as stage:
            sb, pb, sem = allocator(stage)
            by_feature = adj_t_bits[:, :, :].bitcast(fp32).rearrange("p a b -> p (a b)")
            if NT * NW // 2 < 2 * N:
                by_feature = sb("by_feature", [P, 2 * N], fp32)
            x_t = by_feature[:, 0:N]
            max_t = by_feature[:, N:2 * N]
            adj_row = sb("adj_row", [P, N], i32)
            penalty = sb("penalty", [P, N], fp32)
            row_max = sb("row_max", [P, 2], fp32)
            x_tile = sb("x_tile", [P, D], fp32)
            m_tile = sb("m_tile", [P, P], fp32)
            eps = sb("eps0", [P, 1], fp32)
            stats = sb("stats0", [P, 6], fp32)
            moments = sb("moments0", [P, 2], fp32)
            std = sb("std0", [P, 1], fp32)
            turn = pb("turn", [P, P], fp32)
            x_in = sem("gen_x_in")
            x_turned = sem("gen_x_turned")
            x_kept = sem("gen_x_kept")
            row_in = sem("gen_row_in")
            row_done = sem("gen_row_done")
            x_back = sem("gen_x_back")
            m_copied = sem("gen_m_copied")
            m_turned = sem("gen_m_turned")
            var_ready = sem("gen_var_ready")
            std_ready = sem("gen_std_ready")
            x1_ready = sem("gen_x1_ready")
            x1_out = sem("gen_x1_out")
            own = sem("gen_own")

            def tile_rows(t, i):
                return t[bass.ds(i * P, P), :]

            with nc.Block() as block:
                @block.sync
                def _(sync):
                    with sync.If(general(sync) != 0):
                        with sync.Fori(0, NT) as t:
                            sync.wait_ge(x_turned, t)
                            stand_apart(sync)
                            sync.dma_start(x_tile[:, :], tile_rows(x, t)).then_inc(x_in, 16)
                        with sync.Fori(0, N) as i:
                            sync.wait_ge(row_done, i)
                            stand_apart(sync)
                            sync.dma_start(adj_row[:, :], adj[bass.ds(i, 1), :].partition_broadcast(P)).then_inc(row_in, 16)
                        with sync.Fori(0, NT) as t:
                            sync.wait_ge(x1_ready, t)
                            stand_apart(sync)
                            sync.wait_ge(x_turned, NT)
                            sync.dma_start(x_tile[:, :], tile_rows(x, t)).then_inc(x_back, 16)
                            sync.wait_ge(x1_ready, t + 1)
                            stand_apart(sync)
                            sync.dma_start(tile_rows(x1_dram, t), x_tile[:, :]).then_inc(x1_out, 16)
                            sync.wait_ge(x1_out, t * 16 + 16)
                            stand_apart(sync)
                    with sync.Else():
                        sync.nop()

                @block.tensor
                def _(pe):
                    with pe.If(general(pe) != 0):
                        with pe.Fori(0, NT) as t:
                            pe.wait_ge(x_in, t * 16 + 16)
                            pe.wait_ge(x_kept, t)
                            nc.tensor.transpose(turn[:, :], x_tile[:, :], ident[:, :]).then_inc(x_turned, 1)
                        pe.wait_ge(x_kept, NT)
                        with pe.Fori(0, NT) as t:
                            pe.wait_ge(m_copied, t + 1)
                            nc.tensor.transpose(turn[:, :], m_tile[:, :], ident[:, :]).then_inc(m_turned, 1)
                    with pe.Else():
                        pe.nop()

                @block.scalar
                def _(act):
                    with act.If(general(act) != 0):
                        with act.Fori(0, NT) as t:
                            act.wait_ge(x_turned, t + 1)
                            nc.scalar.activation(x_t[:, bass.ds(t * P, P)], turn[:, :], ACT.Copy).then_inc(x_kept, 1)
                        with act.Fori(0, NT) as t:
                            act.wait_ge(var_ready, t + 1)
                            nc.scalar.activation(std[:, :], moments[:, 1:2], ACT.Sqrt, bias=eps[:, :]).then_inc(std_ready, 1)
                    with act.Else():
                        act.nop()

                @block.vector
                def _(dve):
                    with dve.If(general(dve) != 0):
                        v = Chain(dve, own)
                        TS, TT = nc.vector.tensor_scalar, nc.vector.tensor_tensor
                        v(nc.vector.memset(eps[:, :], EPS))
                        dve.wait_ge(x_kept, NT)
                        v.restart()
                        with dve.Fori(0, N) as i:
                            dve.wait_ge(row_in, i * 16 + 16)
                            v(TS(penalty[:, :], adj_row[:, :], 0.0, NEGATIVE, ALU.is_equal, ALU.mult))
                            v.wait()
                            v(nc.vector.tensor_reduce(row_max[:, 0:1], penalty[:, :], AX.X, ALU.max))
                            v.wait()
                            v(TT(penalty[:, :], penalty[:, :], x_t, ALU.add))
                            v(TS(row_max[:, 0:1], row_max[:, 0:1], 0.0, None, ALU.is_equal))
                            v.wait()
                            v(nc.vector.tensor_reduce(row_max[:, 1:2], penalty[:, :], AX.X, ALU.max))
                            v.wait()
                            v(TT(max_t[:, bass.ds(i, 1)], row_max[:, 0:1], row_max[:, 1:2], ALU.mult))
                            v.restart()
                            dve.sem_inc(row_done, 1)
                        with dve.Fori(0, NT) as t:
                            v(nc.vector.tensor_copy(m_tile[:, :], max_t[:, bass.ds(t * P, P)]))
                            v.wait()
                            dve.sem_inc(m_copied, 1)
                            dve.wait_ge(m_turned, t + 1)
                            dve.wait_ge(x_back, t * 16 + 16)
                            v(TT(x_tile[:, :], turn[:, :], x_tile[:, :], ALU.add))
                            v.wait()
                            v(nc.vector.bn_stats(stats[:, :], x_tile[:, :]))
                            v.wait()
                            v(nc.vector.bn_aggr(moments[:, :], stats[:, :]))
                            v.wait()
                            dve.sem_inc(var_ready, 1)
                            dve.wait_ge(std_ready, t + 1)
                            v(nc.vector.reciprocal(row_max[:, 0:1], std[:, :]))
                            v.wait()
                            v(TS(x_tile[:, :], x_tile[:, :], moments[:, 0:1], row_max[:, 0:1], ALU.subtract, ALU.mult))
                            v.wait()
                            hi = feat_hi[:, bass.ds(t, 1), :].rearrange("p o d -> p (o d)")
                            v(TS(hi, x_tile[:, :], X_SCALE, None, ALU.mult))
                            v.wait()
                            v(nc.vector.scalar_tensor_tensor(feat_lo[:, bass.ds(t, 1), :].rearrange("p o d -> p (o d)"),
                                                             x_tile[:, :], X_SCALE, hi, ALU.mult, ALU.subtract))
                            v.restart()
                            dve.sem_inc(x1_ready, 1)
                    with dve.Else():
                        dve.nop()

        with ExitStack() as stage:
            sb, pb, sem = allocator(stage)
            HN = N // 2
            HWD = NW // 2
            BANKS = 8
            BPB = WB // BANKS
            TH = NT // 2
            CH = 4
            CR = CH * P
            NC = NT // CH
            neigh_t = sb("neigh_t", [P, N], fp32)
            open_bits = [sb(f"open_bits{i}", [P, WB, HWD], u16) for i in range(2)]
            w_raw = sb("w_raw", [P, 4 * HK, P], fp32)
            w_t = sb("w_t", [P, 4 * HK, P], fp32)
            x1c = [sb(f"x1c{i}", [P, CH, D], fp32) for i in range(2)]
            x1t = [sb(f"x1t{i}", [P, CR], fp32) for i in range(2)]
            hid = [sb(f"hid{i}", [P, HK, CR], fp32) for i in range(2)]
            gmax = sb("gmax", [P, NC], fp32)
            gm = sb("gm", [P, 4], fp32)
            g_tmp = sb("g_tmp", [P, D], fp32)
            relu_t = [sb(f"relu_t{i}", [P, CR], fp32) for i in range(2)]
            y = [sb(f"y{i}", [P, CH, D], fp32) for i in range(2)]
            gen_adj = sb("gen_adj", [P, CH, P], i32)
            gen_adjf = sb("gen_adjf", [P, CH, P], fp32)
            gen_adj_t = sb("gen_adj_t", [P, CR], fp32)
            gen_feat = sb("gen_feat", [P, D], fp32)
            eps = sb("eps2", [P, 1], fp32)
            stats = sb("stats2", [P, CH, 6], fp32)
            moments = sb("moments2", [P, CH, 2], fp32)
            std = sb("std2", [P, CH], fp32)
            rstd = sb("rstd2", [P, CH], fp32)
            bank = [pb(f"bank{i}", [P, 512], fp32) for i in range(BANKS)]
            assert HK == 2

            def sum_pass(name, evacuate, act_helps):
                opened = sem(f"opened_{name}")
                opened_used = sem(f"opened_used_{name}")
                sums_ready = sem(f"sums_ready_{name}")
                sums_read_v = sem(f"sums_read_v_{name}")
                sums_read_a = sem(f"sums_read_a_{name}")
                step = 2 if act_helps else 1

                block_in = sem(f"gen_in_{name}")
                converted = sem(f"gen_converted_{name}")
                block_turned = sem(f"gen_turned_{name}")
                block_copied = sem(f"gen_copied_{name}")
                multiplied = sem(f"gen_multiplied_{name}")
                summed = sem(f"gen_summed_{name}")
                gen_own = sem(f"gen_own_{name}")

                def general_sync(sync):
                    with sync.Fori(0, NC) as c:
                        with sync.Fori(0, NT) as jb:
                            sync.wait_ge(multiplied, c * NT + jb)
                            stand_apart(sync)
                            sync.dma_start(gen_adj[:, :, :], adj[bass.ds(c * CR, CR), bass.ds(jb * P, P)].rearrange("(s p) j -> p s j", p=P)).then_inc(block_in, 16)

                def general_vector(dve):
                    v = Chain(dve, gen_own)
                    with dve.Fori(0, NC) as c:
                        with dve.Fori(0, NT) as jb:
                            dve.wait_ge(block_in, (c * NT + jb) * 16 + 16)
                            v(nc.vector.tensor_scalar(gen_adjf[:, :, :], gen_adj[:, :, :], 2.0, None, ALU.mult))
                            v(nc.vector.tensor_tensor(gen_feat[:, :], feat_hi[:, bass.ds(jb, 1), :].rearrange("p o d -> p (o d)"),
                                                      feat_lo[:, bass.ds(jb, 1), :].rearrange("p o d -> p (o d)"), ALU.add))
                            v.restart()
                            dve.sem_inc(converted, 1)
                        dve.wait_ge(multiplied, c * NT + NT)
                        v(evacuate(dve, neigh_t[:, bass.ds(c * CR, CR)], bank[1][:, 0:CR]))
                        v.restart()
                        dve.sem_inc(summed, 1)

                def general_scalar(act):
                    with act.Fori(0, NC * NT) as n:
                        act.wait_ge(block_turned, n + 1)
                        nc.scalar.activation(gen_adj_t[:, :], bank[0][:, 0:CR], ACT.Copy).then_inc(block_copied, 1)

                def general_tensor(pe):
                    with pe.Fori(0, NC) as c:
                        def block_of(jb, first, final):
                            pe.wait_ge(converted, c * NT + jb + 1)
                            for s in range(CH):
                                last = nc.tensor.transpose(bank[0][:, s * P:(s + 1) * P], gen_adjf[:, s, :], ident[:, :])
                            last.then_inc(block_turned, 1)
                            pe.wait_ge(block_copied, c * NT + jb + 1)
                            if first:
                                pe.wait_ge(summed, c)
                            nc.tensor.matmul(bank[1][:, 0:CR], gen_feat[:, :], gen_adj_t[:, :], start=first, stop=final).then_inc(multiplied, 1)
                        block_of(0, True, False)
                        with pe.Fori(1, NT - 1) as jb:
                            block_of(jb, False, False)
                        block_of(NT - 1, False, True)

                with nc.Block() as block:
                    @block.sync
                    def _(sync):
                        with sync.If(general(sync) != 0):
                            general_sync(sync)
                        with sync.Else():
                            sync.nop()

                    @block.vector
                    def _(dve):
                        with dve.If(general(dve) == 0):
                            for half in range(2):
                                def open_block(jb, par, skip):
                                    if half and isinstance(jb, int) and jb == 1:
                                        dve.wait_ge(sums_ready, BANKS)
                                    elif not skip:
                                        dve.wait_ge(opened_used, half * (NT - 1) + jb - 1)
                                    src = adj_t_bits[:, bass.ds(jb, 1), half * HWD:(half + 1) * HWD].rearrange("p o w -> p (o w)")
                                    for b in range(WB):
                                        shift = (14 - b, ALU.logical_shift_left) if b <= 14 else (1, ALU.logical_shift_right)
                                        last = nc.vector.tensor_scalar(open_bits[par][:, b, :], src, shift[0], 0x4000, shift[1], ALU.bitwise_and)
                                    last.then_inc(opened, 1)
                                open_block(0, 0, half == 0)
                                open_block(1, 1, half == 0)
                                with dve.Fori(1, NT // 2) as pair:
                                    jb = pair * 2
                                    open_block(jb, 0, False)
                                    open_block(jb + 1, 1, False)
                                for g in range(0, BANKS, step):
                                    dve.wait_ge(sums_ready, half * BANKS + g + 1)
                                    evacuate(dve, rows_of(half, g), bank_rows(g)).then_inc(sums_read_v, 1)
                            dve.wait_ge(sums_read_v, 2 * BANKS // step)
                        with dve.Else():
                            general_vector(dve)

                    @block.scalar
                    def _(act):
                        with act.If(general(act) == 0):
                            for half in range(2):
                                for g in range(1, BANKS, 2) if act_helps else ():
                                    act.wait_ge(sums_ready, half * BANKS + g + 1)
                                    evacuate(act, rows_of(half, g), bank_rows(g)).then_inc(sums_read_a, 1)
                        with act.Else():
                            general_scalar(act)

                    @block.tensor
                    def _(pe):
                        with pe.If(general(pe) == 0):
                            for half in range(2):
                                def multiply(jb, par, first, final):
                                    pe.wait_ge(opened, half * NT + jb + 1)
                                    for part, feat in enumerate((feat_hi, feat_lo)):
                                        for g in range(BANKS):
                                            if first and part == 0 and half:
                                                pe.wait_ge(sums_read_a if act_helps and g % 2 else sums_read_v, g // step + 1)
                                            last = nc.tensor.matmul(
                                                bank[g][:, 0:BPB * HWD], feat[:, bass.ds(jb, 1), :].rearrange("p o d -> p (o d)"),
                                                open_bits[par][:, BPB * g:BPB * (g + 1), :].bitcast(fp16).rearrange("p b w -> p (b w)"),
                                                start=(first and part == 0), stop=(final and part == 1))
                                            if final and part == 1:
                                                last.then_inc(sums_ready, 1)
                                    if not final:
                                        last.then_inc(opened_used, 1)
                                multiply(0, 0, True, False)
                                multiply(1, 1, False, False)
                                with pe.Fori(1, NT // 2 - 1) as pair:
                                    jb = pair * 2
                                    multiply(jb, 0, False, False)
                                    multiply(jb + 1, 1, False, False)
                                multiply(NT - 2, 0, False, False)
                                multiply(NT - 1, 1, False, True)
                        with pe.Else():
                            general_tensor(pe)

            def rows_of(half, g):
                part = neigh_t[:, half * HN:(half + 1) * HN].rearrange("p (w b) -> p b w", b=WB)
                return part[:, BPB * g:BPB * (g + 1), :]

            def bank_rows(g):
                return bank[g][:, 0:BPB * HWD].rearrange("p (b w) -> p b w", b=BPB)

            def take_neighbour_sum(eng, rows, sums):
                if eng.engine == nc.scalar.engine:
                    return nc.scalar.activation(rows, sums, ACT.Copy, scale=0.5 / X_SCALE)
                return nc.vector.tensor_scalar(rows, sums, 0.5 / X_SCALE, None, ALU.mult)

            sum_pass("a", take_neighbour_sum, True)

            w_landed = sem("w_landed")
            w_turned = sem("w_turned")
            w_ready = sem("w_ready")
            x1_landed = [sem(f"x1_landed{i}") for i in range(2)]
            x1_turned = sem("x1_turned")
            x1t_ready = sem("x1t_ready")
            hid_sum = sem("hid_sum")
            hid_ready = sem("hid_ready")
            g_sum = sem("g_sum")
            g_ready = sem("g_ready")
            self_sum = sem("self_sum")
            self_ready = sem("self_ready")
            g_own = sem("g_own")
            gm_ready = sem("gm_ready")
            gm_all = sem("gm_all")
            g32 = [feat_hi[:, :, :].bitcast(fp32), feat_lo[:, :, :].bitcast(fp32)]

            with nc.Block() as block:
                @block.sync
                def _(sync):
                    for n, w in enumerate((w_self_0, w_neigh_0)):
                        sync.dma_start(w_raw[:, n * HK:(n + 1) * HK, :], w.rearrange("(k p) d -> p k d", p=P)).then_inc(w_landed, 16)
                    for n, w in enumerate((w_self_1, w_neigh_1)):
                        sync.dma_start(w_raw[:, (n + 2) * HK:(n + 3) * HK, :], w.rearrange("o (k d) -> o k d", d=P)).then_inc(w_landed, 16)

                    def load(c, par, skip):
                        if not skip:
                            sync.wait_ge(x1_turned, c - 1)
                        sync.dma_start(x1c[par][:, :, :], x1_dram[bass.ds(c * CR, CR), :].rearrange("(s p) d -> p s d", p=P)).then_inc(x1_landed[par], 16)
                    load(0, 0, True)
                    load(1, 1, True)
                    with sync.Fori(1, NC // 2) as pair:
                        c = pair * 2
                        load(c, 0, False)
                        load(c + 1, 1, False)

                @block.tensor
                def _(pe):
                    pe.wait_ge(w_landed, 64)
                    for n in range(4 * HK):
                        last = nc.tensor.transpose(bank[n // 4][:, (n % 4) * P:(n % 4 + 1) * P], w_raw[:, n, :], ident[:, :])
                    last.then_inc(w_turned, 1)
                    pe.wait_ge(w_ready, 2)

                    def chunk(c, par, skip):
                        pe.wait_ge(x1_landed[par], (c // 2 if isinstance(c, int) else c // 2) * 16 + 16)
                        if not skip:
                            pe.wait_ge(x1t_ready, c)
                        for s in range(CH):
                            last = nc.tensor.transpose(bank[0][:, s * P:(s + 1) * P], x1c[par][:, s, :], ident[:, :])
                        last.then_inc(x1_turned, 1)
                        pe.wait_ge(x1t_ready, c + 1)
                        for hh in range(HK):
                            if not skip:
                                pe.wait_ge(hid_ready, c * HK - HK + hh + 1)
                            nc.tensor.matmul(bank[1 + hh][:, 0:CR], w_t[:, hh, :], x1t[par][:, :], start=True, stop=False)
                            nc.tensor.matmul(bank[1 + hh][:, 0:CR], w_t[:, HK + hh, :], neigh_t[:, bass.ds(c * CR, CR)], start=False, stop=True).then_inc(hid_sum, 1)
                        pe.wait_ge(hid_ready, c * HK + HK)
                        if not skip:
                            pe.wait_ge(g_ready, c)
                            pe.wait_ge(self_ready, c)
                        for s in range(CH):
                            for kk in range(HK):
                                last = nc.tensor.matmul(bank[3][:, s * P:(s + 1) * P], hid[par][:, kk, s * P:(s + 1) * P], w_t[:, 3 * HK + kk, :],
                                                        start=(kk == 0), stop=(kk == HK - 1))
                        last.then_inc(g_sum, 1)
                        for kk in range(HK):
                            last = nc.tensor.matmul(bank[4][:, 0:CR], w_t[:, 2 * HK + kk, :], hid[par][:, kk, :], start=(kk == 0), stop=(kk == HK - 1))
                        last.then_inc(self_sum, 1)
                    chunk(0, 0, True)
                    chunk(1, 1, False)
                    with pe.Fori(1, NC // 2) as pair:
                        c = pair * 2
                        chunk(c, 0, False)
                        chunk(c + 1, 1, False)

                @block.scalar
                def _(act):
                    def chunk(c, par, skip):
                        act.wait_ge(x1_turned, c + 1)
                        nc.scalar.activation(x1t[par][:, :], bank[0][:, 0:CR], ACT.Copy).then_inc(x1t_ready, 1)
                        for hh in range(HK):
                            act.wait_ge(hid_sum, c * HK + hh + 1)
                            if not skip:
                                act.wait_ge(self_sum, c - 1)
                            nc.scalar.activation(hid[par][:, hh, :], bank[1 + hh][:, 0:CR], ACT.Relu).then_inc(hid_ready, 1)
                    chunk(0, 0, True)
                    chunk(1, 1, True)
                    with act.Fori(1, NC // 2) as pair:
                        c = pair * 2
                        chunk(c, 0, False)
                        chunk(c + 1, 1, False)

                @block.gpsimd
                def _(pool):
                    pool.wait_ge(gm_ready, 1)
                    pool.partition_all_reduce(gm[:, 1:2], gm[:, 0:1], P, bass.bass_isa.ReduceOp.max).then_inc(gm_all, 1)

                @block.vector
                def _(dve):
                    v = Chain(dve, g_own)
                    dve.wait_ge(w_turned, 1)
                    for n in range(2):
                        nc.vector.tensor_copy(w_t[:, 4 * n:4 * n + 4, :].rearrange("p a b -> p (a b)"), bank[n][:, :]).then_inc(w_ready, 1)

                    def chunk(c):
                        dve.wait_ge(g_sum, c + 1)
                        parts = bank[3][:, :].rearrange("p (s h d) -> p s h d", s=CH, h=2)
                        for hf in range(2):
                            nc.vector.tensor_copy(g32[hf][:, bass.ds(c * CH, CH), :], parts[:, :, hf, :])
                        nc.vector.tensor_reduce(gmax[:, bass.ds(c, 1)], bank[3][:, :], AX.X, ALU.max, apply_absolute_value=True).then_inc(g_ready, 1)
                        dve.wait_ge(self_sum, c + 1)
                        nc.vector.tensor_copy(neigh_t[:, bass.ds(c * CR, CR)], bank[4][:, 0:CR]).then_inc(self_ready, 1)
                    with dve.Fori(0, NC) as c:
                        chunk(c)
                    dve.wait_ge(g_ready, NC)
                    v(nc.vector.tensor_reduce(gm[:, 0:1], gmax[:, :], AX.X, ALU.max))
                    v.wait()
                    v(nc.vector.tensor_scalar(gm[:, 0:1], gm[:, 0:1], 2.0 ** -100, None, ALU.max))
                    v.wait()
                    dve.sem_inc(gm_ready, 1)
                    dve.wait_ge(gm_all, 1)
                    v(nc.vector.tensor_scalar(gm[:, 1:2].bitcast(u32), gm[:, 1:2].bitcast(u32), 0x7F800000, None, ALU.bitwise_and))
                    v.wait()
                    v(nc.vector.tensor_scalar(gm[:, 3:4], gm[:, 1:2], 2.0 ** -15, None, ALU.mult))
                    v(nc.vector.reciprocal(gm[:, 2:3], gm[:, 1:2]))
                    v.wait()
                    v(nc.vector.tensor_scalar(gm[:, 2:3], gm[:, 2:3], 2.0 ** 14, None, ALU.mult))
                    v.wait()
                    v.restart()
                    with dve.Fori(0, NT) as t:
                        for hf in range(2):
                            v(nc.vector.tensor_scalar(g_tmp[:, hf * (D // 2):(hf + 1) * (D // 2)],
                                                      g32[hf][:, bass.ds(t, 1), :].rearrange("p o d -> p (o d)"), gm[:, 2:3], None, ALU.mult))
                        v.wait()
                        hi = feat_hi[:, bass.ds(t, 1), :].rearrange("p o d -> p (o d)")
                        v(nc.vector.tensor_copy(hi, g_tmp[:, :]))
                        v.wait()
                        v(nc.vector.tensor_tensor(feat_lo[:, bass.ds(t, 1), :].rearrange("p o d -> p (o d)"), g_tmp[:, :], hi, ALU.subtract))
                        v.restart()

            def add_self_term(eng, rows, sums):
                return nc.vector.scalar_tensor_tensor(rows, sums, gm[:, 3:4], rows, ALU.mult, ALU.add)

            sum_pass("b", add_self_term, False)

            res_landed = [sem(f"res_landed{i}") for i in range(2)]
            relu_ready = sem("relu_ready")
            turned = sem("turned")
            residual_added = sem("residual_added")
            var2_ready = sem("var2_ready")
            std2_ready = sem("std2_ready")
            fin_own = sem("fin_own")
            out_ready = sem("out_ready")
            out_stored = [sem(f"out_stored{i}") for i in range(2)]
            with nc.Block() as block:
                @block.sync
                def _(sync):
                    def rows(t, c):
                        return t[bass.ds(c * CR, CR), :].rearrange("(s p) d -> p s d", p=P)

                    def load(c, par, skip):
                        if not skip:
                            sync.wait_ge(residual_added, c - 1)
                        sync.dma_start(x1c[par][:, :, :], rows(x1_dram, c)).then_inc(res_landed[par], 16)

                    def store(c, par):
                        sync.wait_ge(out_ready, c + 1)
                        sync.dma_start(rows(out, c), y[par][:, :, :]).then_inc(out_stored[par], 16)
                    load(0, 0, True)
                    load(1, 1, True)
                    with sync.Fori(1, NC // 2) as pair:
                        c = pair * 2
                        load(c, 0, False)
                        store(c - 2, 0)
                        load(c + 1, 1, False)
                        store(c - 1, 1)
                    store(NC - 2, 0)
                    store(NC - 1, 1)
                    for par in range(2):
                        sync.wait_ge(out_stored[par], NC // 2 * 16)

                @block.tensor
                def _(pe):
                    def chunk(c, par, skip):
                        pe.wait_ge(relu_ready, c + 1)
                        if not skip:
                            pe.wait_ge(residual_added, c - 1)
                        for s in range(CH):
                            last = nc.tensor.transpose(bank[par][:, s * P:(s + 1) * P], relu_t[par][:, s * P:(s + 1) * P], ident[:, :])
                        last.then_inc(turned, 1)
                    chunk(0, 0, True)
                    chunk(1, 1, True)
                    with pe.Fori(1, NC // 2) as pair:
                        c = pair * 2
                        chunk(c, 0, False)
                        chunk(c + 1, 1, False)

                @block.scalar
                def _(act):
                    def relu(c, par, skip):
                        if not skip:
                            act.wait_ge(turned, c - 1)
                        nc.scalar.activation(relu_t[par][:, :], neigh_t[:, bass.ds(c * CR, CR)], ACT.Relu).then_inc(relu_ready, 1)

                    def root(c):
                        act.wait_ge(var2_ready, c + 1)
                        nc.scalar.activation(std[:, :], moments[:, :, 1], ACT.Sqrt, bias=eps[:, :]).then_inc(std2_ready, 1)
                    relu(0, 0, True)
                    relu(1, 1, True)
                    with act.Fori(1, NC // 2) as pair:
                        c = pair * 2
                        root(c - 2)
                        relu(c, 0, False)
                        root(c - 1)
                        relu(c + 1, 1, False)
                    root(NC - 2)
                    root(NC - 1)

                @block.vector
                def _(dve):
                    v = Chain(dve, fin_own)
                    v(nc.vector.memset(eps[:, :], EPS))

                    v.restart()

                    def chunk(c, par, skip):
                        yt = y[par]
                        dve.wait_ge(turned, c + 1)
                        dve.wait_ge(res_landed[par], c // 2 * 16 + 16)
                        if not skip:
                            dve.wait_ge(out_stored[par], c // 2 * 16)
                        v(nc.vector.tensor_tensor(yt[:, :, :].rearrange("p s d -> p (s d)"), bank[par][:, 0:CR],
                                                  x1c[par][:, :, :].rearrange("p s d -> p (s d)"), ALU.add))
                        v.wait()
                        dve.sem_inc(residual_added, 1)
                        for s in range(CH):
                            v(nc.vector.bn_stats(stats[:, s, :], yt[:, s, :]))
                        v.wait()
                        for s in range(CH):
                            v(nc.vector.bn_aggr(moments[:, s, :], stats[:, s, :]))
                        v.wait()
                        dve.sem_inc(var2_ready, 1)
                        dve.wait_ge(std2_ready, c + 1)
                        v(nc.vector.reciprocal(rstd[:, :], std[:, :]))
                        v.wait()
                        for s in range(CH):
                            v(nc.vector.tensor_scalar(yt[:, s, :], yt[:, s, :], moments[:, s, 0:1], rstd[:, s:s + 1], ALU.subtract, ALU.mult))
                        v.wait()
                        v.restart()
                        dve.sem_inc(out_ready, 1)
                    chunk(0, 0, True)
                    chunk(1, 1, True)
                    with dve.Fori(1, NC // 2) as pair:
                        c = pair * 2
                        chunk(c, 0, False)
                        chunk(c + 1, 1, False)


def kernel(x, adj, L1_gnn_w_self_0, L1_gnn_w_neigh_0, L1_gnn_w_self_1, L1_gnn_w_neigh_1):
    import numpy as _np
    import concourse.bacc as _bacc
    from concourse.bass_utils import run_bass_kernel_spmd as _run

    given = {
        "x": x, "adj": adj, "w_self_0": L1_gnn_w_self_0, "w_neigh_0": L1_gnn_w_neigh_0,
        "w_self_1": L1_gnn_w_self_1, "w_neigh_1": L1_gnn_w_neigh_1,
    }
    nc = _bacc.Bacc("TRN2", target_bir_lowering=False, num_devices=1)
    arrays, args = {}, []
    for name, a in given.items():
        a = _np.ascontiguousarray(a)
        arrays[f"in_{name}"] = a
        args.append(nc.dram_tensor(f"in_{name}", a.shape, mybir.dt.from_np(a.dtype), kind="ExternalInput").ap())
    out = nc.dram_tensor("out_0", arrays["in_x"].shape, mybir.dt.float32, kind="ExternalOutput").ap()
    graph_max_then_sum_layers(nc, *args, out)
    r = _run(nc, [arrays], core_ids=[0])
    return r.results[0]["out_0"]
```

```python
import concourse.bass as bass
from concourse import mybir
from contextlib import ExitStack


def graph_max_then_sum_layers(nc, x, adj, w_self_0, w_neigh_0, w_self_1, w_neigh_1, out):
    fp32 = mybir.dt.float32
    bf16 = mybir.dt.bfloat16
    fp16 = mybir.dt.float16
    fp8 = mybir.dt.float8e4
    i32 = mybir.dt.int32
    u32 = mybir.dt.uint32
    u16 = mybir.dt.uint16
    ALU = mybir.AluOpType
    ACT = mybir.ActivationFunctionType
    AX = mybir.AxisListType

    N, D = x.shape
    P = 128
    H = w_self_0.shape[0]
    HK = H // P
    NT = N // P
    ST = 8
    NG = NT // ST
    GR = ST * P
    WB = 16
    NW = N // WB
    WT = P // WB
    TOP = 24
    LEVELS = 3
    LC = 32
    C_DEG, C_ROW = 24, 25
    CAPS = [24, 12, 11, 10, 9, 8, 7, 6]
    G_AT = [0, 24, 0, 12, 24, 0, 12, 24]
    REDUCED = [-1, 0, 1, 1, 2, 3, 4, 5]
    MB = 4
    LATE = 5
    EPS = 1e-5
    FP8_ONE = 9
    DEG_BIAS = -7.0 / 16.0
    DEG_BASE = N * DEG_BIAS * DEG_BIAS
    X_SCALE = 4096.0
    NEGATIVE = -3.4028234663852886e38
    DEG_PARTS = 8
    DP = N // DEG_PARTS

    list_dram = nc.dram_tensor("neighbour_lists", (N, LC), u32, kind="Internal").ap()
    max_dram = nc.dram_tensor("neighbour_max", (N, D), fp32, kind="Internal").ap()
    x1_dram = nc.dram_tensor("layer0_out", (N, D), fp32, kind="Internal").ap()

    def group_rows(t, u):
        return t[bass.ds(u * GR, GR), :].rearrange("(s p) d -> p s d", p=P)

    class Chain:

        def __init__(self, eng, sem):
            self.eng, self.sem, self.n = eng, sem, 0

        def __call__(self, ins):
            ins.then_inc(self.sem, 1)
            self.n += 1
            return self.n

        def wait(self, n=None):
            if self.n:
                self.eng.wait_ge(self.sem, self.n if n is None else n)

        def restart(self):
            if self.n:
                self.wait()
                self.eng.sem_clear(self.sem)
            self.n = 0

    def after(eng, sem, value, first):
        if not isinstance(value, int) or value > 0:
            eng.wait_ge(sem, value)

    with ExitStack() as whole:
        def allocator(stack):
            def sb(name, shape, dt):
                return stack.enter_context(nc.sbuf_tensor("sb_" + name, shape, dt))

            def pb(name, shape, dt):
                return stack.enter_context(nc.psum_tensor("ps_" + name, shape, dt))

            def sem(name):
                return stack.enter_context(nc.semaphore(name))
            return sb, pb, sem

        sb, pb, sem = allocator(whole)
        adj_t_bits = sb("adj_t_bits", [P, NT, NW], u16)
        feat_hi = sb("feat_hi", [P, NT, D], fp16)
        feat_lo = sb("feat_lo", [P, NT, D], fp16)
        ident = sb("ident", [P, P], fp32)
        adj_rows = [sb(f"adj_rows{i}", [P, N], i32) for i in range(2)]
        HN = N // 2
        HWD = NW // 2
        BANKS = 8
        BPB = WB // BANKS
        CH = 4
        CR = CH * P
        NC = NT // CH
        neigh_t = adj_rows[0][:, :].bitcast(fp32)
        open_bits = [adj_rows[1][:, :].bitcast(u16)[:, i * WB * HWD:(i + 1) * WB * HWD].rearrange("p (b w) -> p b w", b=WB) for i in range(2)]
        bank = [pb(f"bank{i}", [P, 512], fp32) for i in range(BANKS)]
        flag = sb("flag", [P, 1], fp32)
        flag_all = sb("flag_all", [P, 1], fp32)
        flag_word = sb("flag_word", [P, 1], i32)

        waits = {e: sem(f"waits_{n}") for n, e in enumerate((nc.tensor.engine, nc.scalar.engine, nc.gpsimd.engine, nc.vector.engine, nc.sync.engine))}

        def stand_apart(eng):
            eng.sem_inc(waits[eng.engine], 1)

        opened, opened_used, sums_ready, sums_read_v, sums_read_a, feat_ready = (
            {layer: sem(f"{name}_{layer}") for layer in "ab"}
            for name in ("opened", "opened_used", "sums_ready", "sums_read_v", "sums_read_a", "feat_ready"))

        def open_block(dve, layer, half, jb, par, skip=False):
            if half and isinstance(jb, int) and jb == 1:
                dve.wait_ge(sums_ready[layer], BANKS)
            elif not skip:
                dve.wait_ge(opened_used[layer], half * (NT - 1) + jb - 1)
            src = adj_t_bits[:, bass.ds(jb, 1), half * HWD:(half + 1) * HWD].rearrange("p o w -> p (o w)")
            for b in range(WB):
                shift = (14 - b, ALU.logical_shift_left) if b <= 14 else (1, ALU.logical_shift_right)
                last = nc.vector.tensor_scalar(open_bits[par][:, b, :], src, shift[0], 0x4000, shift[1], ALU.bitwise_and)
            last.then_inc(opened[layer], 1)

        def open_blocks(dve, layer, half, start, end):
            def pair_of(jb, skip):
                for par in range(2):
                    open_block(dve, layer, half, jb + par, par, skip)
            if start == 0 < end:
                pair_of(0, half == 0)
                start = 2
            if end - start == 2:
                pair_of(start, False)
            elif end > start:
                with dve.Fori(start // 2, end // 2) as pair:
                    pair_of(pair * 2, False)

        def multiply_half(pe, layer, half):
            def multiply(jb, par, first, final):
                pe.wait_ge(opened[layer], half * NT + jb + 1)
                for part, feat in enumerate((feat_hi, feat_lo)):
                    for g in range(BANKS):
                        if first and part == 0 and half:
                            if layer == "a" and g % 2:
                                pe.wait_ge(sums_read_a[layer], g // 2 + 1)
                            else:
                                pe.wait_ge(sums_read_v[layer], (g // 2 if layer == "a" else g) + 1)
                        last = nc.tensor.matmul(
                            bank[g][:, 0:BPB * HWD], feat[:, bass.ds(jb, 1), :].rearrange("p o d -> p (o d)"),
                            open_bits[par][:, BPB * g:BPB * (g + 1), :].bitcast(fp16).rearrange("p b w -> p (b w)"),
                            start=(first and part == 0), stop=(final and part == 1))
                        if final and part == 1:
                            last.then_inc(sums_ready[layer], 1)
                if not final:
                    last.then_inc(opened_used[layer], 1)

            def group(u, first, final):
                if not half:
                    pe.wait_ge(feat_ready[layer], u + 1)
                for k in range(ST):
                    multiply(u * ST + k, k % 2, first and k == 0, final and k == ST - 1)
            group(0, True, False)
            if NG > 2:
                with pe.Fori(1, NG - 1) as u:
                    group(u, False, False)
            group(NG - 1, False, True)

        def rows_of(half, g):
            part = neigh_t[:, half * HN:(half + 1) * HN].rearrange("p (w b) -> p b w", b=WB)
            return part[:, BPB * g:BPB * (g + 1), :]

        def bank_rows(g):
            return bank[g][:, 0:BPB * HWD].rearrange("p (b w) -> p b w", b=BPB)

        def take_sums(eng, layer, half, evacuate):
            on_act = eng.engine == nc.scalar.engine
            for g in range(int(on_act), BANKS, 2 if layer == "a" else 1):
                eng.wait_ge(sums_ready[layer], half * BANKS + g + 1)
                evacuate(eng, rows_of(half, g), bank_rows(g)).then_inc((sums_read_a if on_act else sums_read_v)[layer], 1)

        def take_neighbour_sum(eng, rows, sums):
            if eng.engine == nc.scalar.engine:
                return nc.scalar.activation(rows, sums, ACT.Copy, scale=0.5 / X_SCALE)
            return nc.vector.tensor_scalar(rows, sums, 0.5 / X_SCALE, None, ALU.mult)

        with ExitStack() as stage:
            sb, pb, sem = allocator(stage)
            gathered = sb("gathered", [P, 36, D], fp32)
            ones = sb("ones", [P, P], fp32)
            pow2 = sb("pow2", [P, WB], fp32)
            row_pack = sb("row_pack", [P, WB, P], bf16)
            col_terms = sb("col_terms", [P, WT, WB], fp32)
            col_sum = sb("col_sum", [P, WT], fp32)
            col_pack = sb("col_pack", [P, WT], bf16)
            deg_bias = sb("deg_bias", [P, 1], fp32)
            eps = sb("eps", [P, 1], fp32)
            caps = sb("caps", [P, ST], fp32)
            local_row = sb("local_row", [P, ST], i32)
            local_rowf = sb("local_rowf", [P, ST], fp32)
            global_row = sb("global_row", [P, ST], fp32)
            word = sb("word", [P, ST, TOP], fp32)
            word_at = sb("word_at", [P, ST, TOP], u32)
            base = sb("base", [P, ST, TOP], fp32)
            bit = sb("bit", [P, ST, LEVELS, TOP], fp32)
            cand = sb("cand", [P, ST, LEVELS, TOP], fp32)
            near = sb("near", [P, ST, TOP], fp32)
            near_on = sb("near_on", [P, ST, TOP], fp32)
            deg_parts = sb("deg_parts", [P, ST, DEG_PARTS], fp32)
            deg = sb("deg", [P, ST], fp32)
            listed = sb("listed", [P, ST], fp32)
            key = sb("key", [P, ST], fp32)
            key_diag = sb("key_diag", [P, ST // 2, P], fp32)
            rest = key_diag[:, :, :].rearrange("p s q -> p (s q)")[:, 0:NW]
            rank_junk = sb("rank_junk", [P, GR], mybir.dt.uint8)
            rank = sb("rank", [P, ST], fp32)
            rank_u = sb("rank_u", [P, ST], u32)
            record = sb("record", [P, ST, LC], u32)
            lists = [sb(f"lists{i}", [P, ST, LC], u32) for i in range(2)]
            degrees = sb("degrees", [P, ST], u32)
            has_near = sb("has_near", [P, ST], fp32)
            over = sb("over", [P, ST], fp32)
            over1 = sb("over1", [P, 1], fp32)
            near_max = [sb(f"near_max{i}", [P, D], fp32) for i in range(MB)]
            x_nat = [f[:, NT - ST:NT, :].bitcast(fp32).rearrange("p s (h d) -> p (s h d)", h=1).rearrange("p (s d) -> p s d", d=D)
                     for f in (feat_hi, feat_lo)]
            m_nat = sb("m_nat", [P, ST, D], fp32)
            stats = sb("stats", [P, ST, 6], fp32)
            moments = sb("moments", [P, ST, 2], fp32)
            std = sb("std", [P, ST], fp32)
            rstd = sb("rstd", [P, ST], fp32)
            WORD_BANKS = 4
            NORM_AT = 4
            KEYS_AT = 2
            pw = [bank[i][:, 0:NW] for i in range(WORD_BANKS)]
            pt = [bank[4 + i][:, 0:NT * WT] for i in range(2)]
            pk = [bank[6 + i][:, 0:GR // 2] for i in range(2)]

            deg_junk = [sb(f"deg_junk{i}", [P, DP], fp8) for i in range(2)]

            adj_landed = [sem(f"adj_landed{i}") for i in range(2)]
            const_a = sem("const_a")
            const_v = sem("const_v")
            words_ready = sem("words_ready")
            words_read = sem("words_read")
            words_t_ready = sem("words_t_ready")
            words_t_read = sem("words_t_read")
            deg_ready = sem("deg_ready")
            deg_read = sem("deg_read")
            diag_ready = sem("diag_ready")
            keys_ready = sem("keys_ready")
            keys_read = sem("keys_read")
            vec = sem("vec")
            act_own = sem("act_own")
            pool_own = sem("pool_own")
            records_ready = sem("records_ready")
            records_stored = sem("records_stored")
            lists_landed = sem("lists_landed")
            gather_landed = [sem(f"gather_landed{s}") for s in range(ST)]
            degrees_copied = sem("degrees_copied")
            max_ready = sem("max_ready")
            max_stored = [sem(f"max_stored{i}") for i in range(MB)]
            nat_landed = sem("nat_landed")
            var_ready = sem("var_ready")
            std_ready = sem("std_ready")
            x1_ready = sem("x1_ready")
            x1_stored = sem("x1_stored")
            block = stage.enter_context(nc.Block())

            @block.sync
            def _(sync):
                def group(u):
                    for t in range(ST):
                        after(sync, words_t_ready, u * ST + t - 1, u)
                        after(sync, deg_ready, u * ST + t - 1, u)
                        sync.dma_start(adj_rows[t % 2][:, :], adj[bass.ds((u * ST + t) * P, P), :]).then_inc(adj_landed[t % 2], 16)
                group(0)
                if NG > 1:
                    with sync.Fori(1, NG) as u:
                        group(u)

            @block.tensor
            def _(pe):
                pe.wait_ge(const_v, 1)

                def keys(u):
                    for half in range(2):
                        pe.wait_ge(diag_ready, u * 2 + half + 1)
                        nc.tensor.matmul(pk[half], ones[:, :], key_diag[:, :, :].rearrange("p s q -> p (s q)"), start=True, stop=True).then_inc(keys_ready, 1)

                def group(u, sorted_group):
                    for t in range(ST):
                        if t == KEYS_AT and sorted_group is not None:
                            keys(sorted_group)
                        by_byte = adj_rows[t % 2][:, :].bitcast(fp8)
                        by_word = by_byte.rearrange("p (c k b) -> p c k b", k=WB, b=4)
                        by_block = by_byte.rearrange("p (j q b) -> p j q b", q=P, b=4)
                        pe.wait_ge(adj_landed[t % 2], (u * (ST // 2) + t // 2 + 1) * 16)
                        after(pe, words_read, u * ST + t - WORD_BANKS + 1, u)
                        stand_apart(pe)
                        for k in range(WB):
                            last = nc.tensor.matmul(pw[t % WORD_BANKS], row_pack[:, k, :], by_word[:, :, k, 0], start=(k == 0), stop=(k == WB - 1))
                        last.then_inc(words_ready, 1)
                        after(pe, words_t_read, u * ST + t - 1, u)
                        stand_apart(pe)
                        for j in range(NT):
                            last = nc.tensor.matmul(pt[t % 2][:, j * WT:(j + 1) * WT], by_block[:, j, :, 0], col_pack[:, :], start=True, stop=True)
                        last.then_inc(words_t_ready, 1)
                group(0, None)
                if NG > 1:
                    with pe.Fori(1, NG) as u:
                        group(u, u - 1)
                keys(NG - 1)
                pe.wait_ge(words_t_read, NT)
                pe.wait_ge(records_ready, NG)
                for half in range(2):
                    multiply_half(pe, "a", half)

            @block.scalar
            def _(act):
                a = Chain(act, act_own)
                act.wait_ge(const_a, 1)

                def root(norm):
                    act.wait_ge(var_ready, norm + 1)
                    nc.scalar.activation(std[:, :], moments[:, :, 1], ACT.Sqrt, bias=eps[:, :]).then_inc(std_ready, 1)

                def group(u, norm):
                    for t in range(ST):
                        act.wait_ge(adj_landed[t % 2], (u * (ST // 2) + t // 2 + 1) * 16)
                        if t == 0:
                            after(act, deg_read, u, u)
                        stand_apart(act)
                        for c in range(DEG_PARTS):
                            if a.n >= 2:
                                a.wait(a.n - 1)
                            a(nc.scalar.activation(deg_junk[c % 2][:, :], adj_rows[t % 2][:, c * DP:(c + 1) * DP], ACT.Square,
                                                   bias=deg_bias[:, :], accum_out=deg_parts[:, t, c:c + 1], saturate=False))
                        a.wait()
                        act.sem_inc(deg_ready, 1)
                        act.wait_ge(words_t_ready, u * ST + t + 1)
                        nc.scalar.activation(adj_t_bits[:, :, bass.ds((u * ST + t) * WT, WT)],
                                             pt[t % 2].rearrange("p (j w) -> p j w", w=WT), ACT.Copy).then_inc(words_t_read, 1)
                        if t == NORM_AT and norm is not None:
                            root(norm)
                    a.restart()
                for u in range(min(3, NG)):
                    group(u, None)
                if NG > 3:
                    with act.Fori(3, NG) as u:
                        group(u, u - 3)
                for norm in range(max(0, NG - 3), NG):
                    root(norm)
                for half in range(2):
                    take_sums(act, "a", half, take_neighbour_sum)

            @block.gpsimd
            def _(pool):
                pool.memset(ident[:, :], 0.0).then_inc(pool_own, 1)
                pool.wait_ge(pool_own, 1)
                pool.affine_select(out=ident[:, :], in_=ident[:, :], compare_op=ALU.not_equal, fill=1.0, base=0,
                                   pattern=[[-1, P]], channel_multiplier=1).then_inc(pool_own, 1)
                pool.memset(ones[:, :], 1.0).then_inc(pool_own, 1)
                for k in range(WB):
                    pool.memset(pow2[:, k:k + 1], 2.0 ** (k + FP8_ONE)).then_inc(pool_own, 1)
                for s in range(ST):
                    pool.memset(caps[:, s:s + 1], float(CAPS[s])).then_inc(pool_own, 1)
                pool.memset(deg_bias[:, :], DEG_BIAS).then_inc(pool_own, 1)
                pool.memset(eps[:, :], EPS).then_inc(pool_own, 1)
                pool.iota(local_row[:, :], [[P, ST]], channel_multiplier=1).then_inc(pool_own, 1)
                pool.memset(flag[:, :], 0.0).then_inc(pool_own, 1)
                done = 2 + 1 + WB + ST + 4
                pool.wait_ge(pool_own, done)
                pool.sem_inc(const_a, 1)

                def store_lists(u):
                    pool.wait_ge(records_ready, u + 1)
                    stand_apart(pool)
                    for t in range(ST):
                        pool.indirect_dma_start(list_dram, bass.IndirectOffsetOnAxis(ap=rank_u[:, t:t + 1], axis=0),
                                                record[:, t, :], None, bounds_check=N - 1, oob_is_err=False).then_inc(records_stored, 16)

                def load_natural(u):
                    for i in range(MB):
                        pool.wait_ge(max_stored[i], (u + 1) * (ST // MB) * 16)
                        stand_apart(pool)
                    after(pool, x1_stored, u * 16, u)
                    stand_apart(pool)
                    pool.dma_start(m_nat[:, :, :], group_rows(max_dram, u)).then_inc(nat_landed, 16)
                    for half in range(2):
                        pool.dma_start(x_nat[half], group_rows(x, u)[:, half * ST // 2:(half + 1) * ST // 2, :]).then_inc(nat_landed, 16)

                def store_x1(u):
                    pool.wait_ge(x1_ready, u + 1)
                    stand_apart(pool)
                    pool.dma_start(group_rows(x1_dram, u), m_nat[:, :, :]).then_inc(x1_stored, 16)

                def store_max(u, s, par):
                    pool.wait_ge(max_ready, u * ST + s + 1)
                    stand_apart(pool)
                    pool.indirect_dma_start(max_dram, bass.IndirectOffsetOnAxis(ap=lists[par][:, s, C_ROW:C_ROW + 1], axis=0),
                                            near_max[s % MB][:, :], None, bounds_check=N - 1, oob_is_err=False).then_inc(max_stored[s % MB], 16)

                def load_lists(u, par):
                    pool.wait_ge(records_stored, (u + 1) * ST * 16)
                    stand_apart(pool)
                    if not isinstance(u, int) or u > 1:
                        for i in range(MB):
                            pool.wait_ge(max_stored[i], (u - 1) * (ST // MB) * 16)
                            stand_apart(pool)
                    pool.dma_start(lists[par][:, :, :], group_rows(list_dram, u)).then_inc(lists_landed, 16)

                def copy_degrees(u, par):
                    pool.wait_ge(lists_landed, (u + 1) * 16)
                    stand_apart(pool)
                    after(pool, max_ready, u * ST - ST + 1, u)
                    stand_apart(pool)
                    pool.tensor_copy(degrees[:, :], lists[par][:, :, C_DEG]).then_inc(degrees_copied, 1)
                    pool.wait_ge(degrees_copied, u + 1)
                    stand_apart(pool)

                def gather(u, s, par):
                    after(pool, max_ready, u * ST + REDUCED[s], u)
                    stand_apart(pool)
                    for k in range(CAPS[s]):
                        pool.indirect_dma_start(gathered[:, G_AT[s] + k, :], None, x,
                                                bass.IndirectOffsetOnAxis(ap=lists[par][:, s, k:k + 1], axis=0),
                                                bounds_check=N - 1, oob_is_err=False).then_inc(gather_landed[s], 16)

                def group(u, par, before, stored, following):
                    for s in range(ST):
                        if s == LATE and following:
                            store_lists(u + 1)
                        gather(u, s, par)
                        if s < 2:
                            if before is not None:
                                store_max(before, ST - 2 + s, 1 - par)
                        else:
                            store_max(u, s - 2, par)
                        if s == 0 and stored is not None:
                            store_x1(stored)
                        if s == 3 and before is not None:
                            load_natural(before)
                        if s == LATE and following:
                            load_lists(u + 1, 1 - par)
                    if following:
                        copy_degrees(u + 1, 1 - par)

                store_lists(0)
                load_lists(0, 0)
                copy_degrees(0, 0)
                group(0, 0, None, None, True)
                if NG > 2:
                    group(1, 1, 0, None, True)
                    if NG > 4:
                        with pool.Fori(1, NG // 2 - 1) as pair:
                            for par in range(2):
                                u = pair * 2 + par
                                group(u, par, u - 1, u - 2, True)
                    group(NG - 2, 0, NG - 3, NG - 4, True)
                group(NG - 1, 1, NG - 2, NG - 3 if NG > 2 else None, False)
                for s in range(ST - 2, ST):
                    store_max(NG - 1, s, 1)
                store_x1(NG - 2)
                load_natural(NG - 1)
                store_x1(NG - 1)
                pool.wait_ge(x1_stored, NG * 16)
                stand_apart(pool)

            @block.vector
            def _(dve):
                v = Chain(dve, vec)
                TT, TS, STT = nc.vector.tensor_tensor, nc.vector.tensor_scalar, nc.vector.scalar_tensor_tensor
                dve.wait_ge(const_a, 1)
                v(TT(row_pack[:, :, :], ident[:, :].unsqueeze(1).to_broadcast([P, WB, P]),
                     pow2[:, :].unsqueeze(2).to_broadcast([P, WB, P]), ALU.mult))
                v(TT(col_terms[:, :, :], ident[:, :].rearrange("p (m k) -> p m k", k=WB),
                     pow2[:, :].unsqueeze(1).to_broadcast([P, WT, WB]), ALU.mult))
                v(nc.vector.tensor_copy(local_rowf[:, :], local_row[:, :]))
                v(nc.vector.tensor_copy(global_row[:, :], local_row[:, :]))
                v(nc.vector.memset(record[:, :, :].bitcast(fp32), 0.0))
                v.wait()
                v(nc.vector.tensor_reduce(col_sum[:, :], col_terms[:, :, :], AX.X, ALU.add))
                v.wait()
                v(nc.vector.tensor_copy(col_pack[:, :], col_sum[:, :]))
                v.wait()
                dve.sem_inc(const_v, 1)

                def extract(u, t):
                    dve.wait_ge(words_ready, u * ST + t + 1)
                    stand_apart(dve)
                    source = pw[t % WORD_BANKS]
                    for r in range(TOP // 8):
                        eight = word[:, t, 8 * r:8 * r + 8]
                        v(nc.vector.max(eight, source))
                        v.wait()
                        v(nc.vector.max_index(word_at[:, t, 8 * r:8 * r + 8], eight, source))
                        if r < TOP // 8 - 1:
                            v(nc.vector.match_replace(rest, eight, source, 0.0))
                            source = rest
                            if r == 0:
                                v.wait()
                                dve.sem_inc(words_read, 1)
                        v.wait()

                def neighbours(u):
                    dve.wait_ge(deg_ready, (u + 1) * ST)
                    v(nc.vector.tensor_reduce(deg[:, :], deg_parts[:, :, :], AX.X, ALU.add))
                    v.wait()
                    dve.sem_inc(deg_read, 1)
                    b = [bit[:, :, lv, :] for lv in range(LEVELS)]
                    left = word[:, :, :]
                    v(TS(base[:, :, :], word_at[:, :, :], float(WB), float(1 - 127), ALU.mult, ALU.add))
                    for lv in range(LEVELS):
                        v(TS(b[lv].bitcast(u32), left.bitcast(u32), 0x7F800000, None, ALU.bitwise_and))
                        v.wait()
                        if lv < LEVELS - 1:
                            v(TT(left, left, b[lv], ALU.subtract))
                            v.wait()
                    v(TS(cand[:, :, :, :].bitcast(u32), bit[:, :, :, :].bitcast(u32), 23, None, ALU.logical_shift_right))
                    v.wait()
                    v(TT(cand[:, :, :, :], cand[:, :, :, :].bitcast(u32), base[:, :, :].unsqueeze(2).to_broadcast([P, ST, LEVELS, TOP]), ALU.add))
                    v.wait()
                    v(STT(cand[:, :, :, :], bit[:, :, :, :], 0.0, cand[:, :, :, :], ALU.is_gt, ALU.mult))
                    v.wait()
                    for r in range(TOP // 8):
                        for t in range(ST):
                            v(nc.vector.max(near[:, t, 8 * r:8 * r + 8], cand[:, t, :, :].rearrange("p l k -> p (l k)")))
                        v.wait()
                        if r < TOP // 8 - 1:
                            for t in range(ST):
                                flat = cand[:, t, :, :].rearrange("p l k -> p (l k)")
                                v(nc.vector.match_replace(flat, near[:, t, 8 * r:8 * r + 8], flat, 0.0))
                            v.wait()
                    v(TS(near_on[:, :, :], near[:, :, :], 0.0, None, ALU.is_gt))
                    v(TS(deg[:, :], deg[:, :], -DEG_BASE, 8.0, ALU.add, ALU.mult))
                    v.wait()
                    v(nc.vector.tensor_reduce(listed[:, :], near_on[:, :, :], AX.X, ALU.add))
                    v.wait()
                    v(TT(over[:, :], deg[:, :], listed[:, :], ALU.not_equal))
                    v(TS(key[:, :], deg[:, :], 64.0, float(GR), ALU.min, ALU.mult))
                    v.wait()
                    v(nc.vector.tensor_reduce(over1[:, :], over[:, :], AX.X, ALU.max))
                    v(TT(key[:, :], key[:, :], local_rowf[:, :], ALU.add))
                    v.wait()
                    v(TT(flag[:, :], flag[:, :], over1[:, :], ALU.max))

                def sort_rows(u):
                    for half in range(2):
                        if half:
                            dve.wait_ge(keys_ready, u * 2 + 1)
                        n = ST // 2
                        v(TT(key_diag[:, :, :], ident[:, :].unsqueeze(1).to_broadcast([P, n, P]),
                             key[:, half * n:half * n + n].unsqueeze(2).to_broadcast([P, n, P]), ALU.mult))
                        v.wait()
                        dve.sem_inc(diag_ready, 1)
                    v(TS(near_on[:, :, :], near_on[:, :, :], -1.0, 1.0, ALU.mult, ALU.add))
                    v.wait()
                    v(TT(near_on[:, :, :], near_on[:, :, :], near[:, :, 0:1].to_broadcast([P, ST, TOP]), ALU.mult))
                    v.wait()
                    v(TT(near[:, :, :], near[:, :, :], near_on[:, :, :], ALU.add))
                    after(dve, records_stored, u * ST * 16, u)
                    v.wait()
                    v(TS(near[:, :, :], near[:, :, :], 1.0, float(N), ALU.max, ALU.min))
                    v.wait()
                    v(TS(record[:, :, 0:TOP], near[:, :, :], -1.0, None, ALU.add))
                    v(TS(record[:, :, C_DEG], deg[:, :], 64.0, None, ALU.min))
                    v(nc.vector.tensor_copy(record[:, :, C_ROW], global_row[:, :]))
                    for half in range(2):
                        dve.wait_ge(keys_ready, u * 2 + half + 1)
                    for t in range(ST):
                        for half in range(2):
                            v(TS(rank_junk[:, half * GR // 2:(half + 1) * GR // 2], pk[half], key[:, t:t + 1],
                                 0.0 if half == 0 else rank[:, t:t + 1], ALU.is_gt, ALU.add, accum_out=rank[:, t:t + 1]))
                            if half == 0:
                                v.wait()
                    v.wait()
                    v(TT(rank[:, :], rank[:, :], global_row[:, :], ALU.add))
                    v.wait()
                    v(TT(rank_u[:, :], rank[:, :], local_rowf[:, :], ALU.subtract))
                    v.wait()
                    v(TS(global_row[:, :], global_row[:, :], float(GR), None, ALU.add))
                    dve.sem_inc(records_ready, 1)

                def reduce_max(u, s):
                    dve.wait_ge(gather_landed[s], (u + 1) * CAPS[s] * 16)
                    if s == 0:
                        v(TS(has_near[:, :], degrees[:, :], 0.0, None, ALU.is_gt))
                        v(TT(over[:, :], degrees[:, :], caps[:, :], ALU.is_gt))
                        v.wait()
                        v(nc.vector.tensor_reduce(over1[:, :], over[:, :], AX.X, ALU.max))
                        v.wait()
                        v(TT(flag[:, :], flag[:, :], over1[:, :], ALU.max))
                    after(dve, max_stored[s % MB], (u * (ST // MB) + s // MB) * 16, u)
                    v(nc.vector.tensor_reduce(near_max[s % MB][:, :], gathered[:, G_AT[s]:G_AT[s] + CAPS[s], :].rearrange("p k d -> p d k"), AX.X, ALU.max))
                    v.wait()
                    v(TS(near_max[s % MB][:, :], near_max[s % MB][:, :], has_near[:, s:s + 1], None, ALU.mult))
                    v.wait()
                    dve.sem_inc(max_ready, 1)

                def take_moments(u):
                    dve.wait_ge(nat_landed, (u + 1) * 48)
                    for half in range(2):
                        part = m_nat[:, half * ST // 2:(half + 1) * ST // 2, :]
                        v(TT(part, part, x_nat[half], ALU.add))
                    v.wait()
                    for s in range(ST):
                        v(nc.vector.bn_stats(stats[:, s, :], m_nat[:, s, :]))
                    v.wait()
                    for s in range(ST):
                        v(nc.vector.bn_aggr(moments[:, s, :], stats[:, s, :]))
                    v.wait()
                    dve.sem_inc(var_ready, 1)

                def scale_rows(u):
                    dve.wait_ge(std_ready, u + 1)
                    v(nc.vector.reciprocal(rstd[:, :], std[:, :]))
                    v.wait()
                    for s in range(ST):
                        v(TS(m_nat[:, s, :], m_nat[:, s, :], moments[:, s, 0:1], rstd[:, s:s + 1], ALU.subtract, ALU.mult))
                    v.wait()
                    dve.sem_inc(x1_ready, 1)
                    hi = feat_hi[:, bass.ds(u * ST, ST), :]
                    v(TS(hi, m_nat[:, :, :], X_SCALE, None, ALU.mult))
                    v.wait()
                    v(STT(feat_lo[:, bass.ds(u * ST, ST), :], m_nat[:, :, :], X_SCALE, hi, ALU.mult, ALU.subtract))
                    v.wait()
                    dve.sem_inc(feat_ready["a"], 1)

                def normalise(u):
                    take_moments(u)
                    scale_rows(u)

                def group(u, late, reduced, normed):
                    turns = {1: ((late, 3),), 2: ((late, 4),), 5: ((late, 5),), 6: ((late, 6),), 7: ((late, 7),)}

                    def reduce_if(g, s):
                        if g is not None:
                            reduce_max(g, s)
                    for t in range(ST):
                        extract(u, t)
                        if t == NORM_AT - 2 and normed is not None:
                            take_moments(normed)
                        if t == NORM_AT - 1 and normed is not None:
                            scale_rows(normed)
                        for turn in turns.get(t, ()):
                            reduce_if(*turn)
                    neighbours(u)
                    reduce_if(reduced, 0)
                    sort_rows(u)
                    reduce_if(reduced, 1)
                    reduce_if(reduced, 2)
                    v.restart()

                v.restart()
                group(0, None, None, None)
                group(1, None, 0, None)
                if NG > 2:
                    group(2, 0, 1, None)
                if NG > 3:
                    with dve.Fori(3, NG) as u:
                        group(u, u - 2, u - 1, u - 3)

                dve.wait_ge(words_t_read, NT)
                dve.wait_ge(words_t_ready, NT)
                dve.wait_ge(deg_ready, NT)
                LAST, BEFORE = NG - 1, NG - 2
                last_steps = [(4, normalise, NG - 3), (2, reduce_max, BEFORE, 3), (4, reduce_max, BEFORE, 4), (8, reduce_max, BEFORE, 5), (10, reduce_max, BEFORE, 6), (12, reduce_max, BEFORE, 7),
                              (20, reduce_max, LAST, 0), (22, reduce_max, LAST, 1), (26, reduce_max, LAST, 2), (28, reduce_max, LAST, 3),
                              (30, normalise, BEFORE), (32, reduce_max, LAST, 4), (34, reduce_max, LAST, 5), (36, reduce_max, LAST, 6),
                              (40, reduce_max, LAST, 7), (44, normalise, LAST)]
                at = 0
                for n, (place, what, *of) in enumerate(last_steps):
                    if of[0] < 0:
                        continue
                    place = min([place] + [g[0] * ST for _, w, *g in last_steps[n:] if w is normalise])
                    open_blocks(dve, "a", 0, at, max(at, place))
                    at = max(at, place)
                    what(*of)
                open_blocks(dve, "a", 0, at, NT)
                take_sums(dve, "a", 0, take_neighbour_sum)
                open_blocks(dve, "a", 1, 0, NT)
                take_sums(dve, "a", 1, take_neighbour_sum)
                dve.wait_ge(sums_read_v["a"], BANKS)
                v.restart()

        flag_reduced = sem("flag_reduced")
        flag_own = sem("flag_own")
        with nc.Block() as block:
            @block.gpsimd
            def _(pool):
                pool.partition_all_reduce(flag_all[:, :], flag[:, :], P, bass.bass_isa.ReduceOp.max).then_inc(flag_reduced, 1)

            @block.vector
            def _(dve):
                dve.wait_ge(flag_reduced, 1)
                nc.vector.tensor_scalar(flag_all[:, :], flag_all[:, :], 0.0, None, ALU.is_gt).then_inc(flag_own, 1)
                dve.wait_ge(flag_own, 1)
                nc.vector.tensor_copy(flag_word[:, :], flag_all[:, :]).then_inc(flag_own, 1)
                dve.wait_ge(flag_own, 2)

        def general(eng):
            return eng.value_load(flag_word[0:1, 0:1], min_val=0, max_val=1)

        with ExitStack() as stage:
            sb, pb, sem = allocator(stage)
            by_feature = adj_t_bits[:, :, :].bitcast(fp32).rearrange("p a b -> p (a b)")
            if NT * NW // 2 < 2 * N:
                by_feature = sb("by_feature", [P, 2 * N], fp32)
            x_t = by_feature[:, 0:N]
            max_t = by_feature[:, N:2 * N]
            adj_row = adj_rows[0]
            penalty = adj_rows[1][:, :].bitcast(fp32)
            row_max = sb("row_max", [P, 2], fp32)
            x_tile = sb("x_tile", [P, D], fp32)
            m_tile = sb("m_tile", [P, P], fp32)
            eps = sb("eps0", [P, 1], fp32)
            stats = sb("stats0", [P, 6], fp32)
            moments = sb("moments0", [P, 2], fp32)
            std = sb("std0", [P, 1], fp32)
            turn = bank[0][:, 0:P]
            x_in = sem("gen_x_in")
            x_turned = sem("gen_x_turned")
            x_kept = sem("gen_x_kept")
            row_in = sem("gen_row_in")
            row_done = sem("gen_row_done")
            x_back = sem("gen_x_back")
            m_copied = sem("gen_m_copied")
            m_turned = sem("gen_m_turned")
            var_ready = sem("gen_var_ready")
            std_ready = sem("gen_std_ready")
            x1_ready = sem("gen_x1_ready")
            x1_out = sem("gen_x1_out")
            own = sem("gen_own")

            def tile_rows(t, i):
                return t[bass.ds(i * P, P), :]

            with nc.Block() as block:
                @block.sync
                def _(sync):
                    with sync.If(general(sync) != 0):
                        with sync.Fori(0, NT) as t:
                            sync.wait_ge(x_turned, t)
                            stand_apart(sync)
                            sync.dma_start(x_tile[:, :], tile_rows(x, t)).then_inc(x_in, 16)
                        with sync.Fori(0, N) as i:
                            sync.wait_ge(row_done, i)
                            stand_apart(sync)
                            sync.dma_start(adj_row[:, :], adj[bass.ds(i, 1), :].partition_broadcast(P)).then_inc(row_in, 16)
                        with sync.Fori(0, NT) as t:
                            sync.wait_ge(x1_ready, t)
                            stand_apart(sync)
                            sync.wait_ge(x_turned, NT)
                            sync.dma_start(x_tile[:, :], tile_rows(x, t)).then_inc(x_back, 16)
                            sync.wait_ge(x1_ready, t + 1)
                            stand_apart(sync)
                            sync.dma_start(tile_rows(x1_dram, t), x_tile[:, :]).then_inc(x1_out, 16)
                            sync.wait_ge(x1_out, t * 16 + 16)
                            stand_apart(sync)
                    with sync.Else():
                        sync.nop()

                @block.tensor
                def _(pe):
                    with pe.If(general(pe) != 0):
                        with pe.Fori(0, NT) as t:
                            pe.wait_ge(x_in, t * 16 + 16)
                            pe.wait_ge(x_kept, t)
                            nc.tensor.transpose(turn, x_tile[:, :], ident[:, :]).then_inc(x_turned, 1)
                        pe.wait_ge(x_kept, NT)
                        with pe.Fori(0, NT) as t:
                            pe.wait_ge(m_copied, t + 1)
                            nc.tensor.transpose(turn, m_tile[:, :], ident[:, :]).then_inc(m_turned, 1)
                    with pe.Else():
                        pe.nop()

                @block.scalar
                def _(act):
                    with act.If(general(act) != 0):
                        with act.Fori(0, NT) as t:
                            act.wait_ge(x_turned, t + 1)
                            nc.scalar.activation(x_t[:, bass.ds(t * P, P)], turn, ACT.Copy).then_inc(x_kept, 1)
                        with act.Fori(0, NT) as t:
                            act.wait_ge(var_ready, t + 1)
                            nc.scalar.activation(std[:, :], moments[:, 1:2], ACT.Sqrt, bias=eps[:, :]).then_inc(std_ready, 1)
                    with act.Else():
                        act.nop()

                @block.vector
                def _(dve):
                    with dve.If(general(dve) != 0):
                        v = Chain(dve, own)
                        TS, TT = nc.vector.tensor_scalar, nc.vector.tensor_tensor
                        v(nc.vector.memset(eps[:, :], EPS))
                        dve.wait_ge(x_kept, NT)
                        v.restart()
                        with dve.Fori(0, N) as i:
                            dve.wait_ge(row_in, i * 16 + 16)
                            v(TS(penalty, adj_row[:, :], 0.0, NEGATIVE, ALU.is_equal, ALU.mult))
                            v.wait()
                            v(nc.vector.tensor_reduce(row_max[:, 0:1], penalty, AX.X, ALU.max))
                            v.wait()
                            v(TT(penalty, penalty, x_t, ALU.add))
                            v(TS(row_max[:, 0:1], row_max[:, 0:1], 0.0, None, ALU.is_equal))
                            v.wait()
                            v(nc.vector.tensor_reduce(row_max[:, 1:2], penalty, AX.X, ALU.max))
                            v.wait()
                            v(TT(max_t[:, bass.ds(i, 1)], row_max[:, 0:1], row_max[:, 1:2], ALU.mult))
                            v.restart()
                            dve.sem_inc(row_done, 1)
                        with dve.Fori(0, NT) as t:
                            v(nc.vector.tensor_copy(m_tile[:, :], max_t[:, bass.ds(t * P, P)]))
                            v.wait()
                            dve.sem_inc(m_copied, 1)
                            dve.wait_ge(m_turned, t + 1)
                            dve.wait_ge(x_back, t * 16 + 16)
                            v(TT(x_tile[:, :], turn, x_tile[:, :], ALU.add))
                            v.wait()
                            v(nc.vector.bn_stats(stats[:, :], x_tile[:, :]))
                            v.wait()
                            v(nc.vector.bn_aggr(moments[:, :], stats[:, :]))
                            v.wait()
                            dve.sem_inc(var_ready, 1)
                            dve.wait_ge(std_ready, t + 1)
                            v(nc.vector.reciprocal(row_max[:, 0:1], std[:, :]))
                            v.wait()
                            v(TS(x_tile[:, :], x_tile[:, :], moments[:, 0:1], row_max[:, 0:1], ALU.subtract, ALU.mult))
                            v.wait()
                            hi = feat_hi[:, bass.ds(t, 1), :].rearrange("p o d -> p (o d)")
                            v(TS(hi, x_tile[:, :], X_SCALE, None, ALU.mult))
                            v.wait()
                            v(nc.vector.scalar_tensor_tensor(feat_lo[:, bass.ds(t, 1), :].rearrange("p o d -> p (o d)"),
                                                             x_tile[:, :], X_SCALE, hi, ALU.mult, ALU.subtract))
                            v.restart()
                            dve.sem_inc(x1_ready, 1)
                    with dve.Else():
                        dve.nop()

        with ExitStack() as stage:
            sb, pb, sem = allocator(stage)
            w_raw = sb("w_raw", [P, 4 * HK, P], fp32)
            w_t = sb("w_t", [P, 4 * HK, P], fp32)
            x1c = [sb(f"x1c{i}", [P, CH, D], fp32) for i in range(2)]
            x1t = [sb(f"x1t{i}", [P, CR], fp32) for i in range(2)]
            hid = [sb(f"hid{i}", [P, HK, CR], fp32) for i in range(2)]
            gmax = sb("gmax", [P, NC], fp32)
            gm = sb("gm", [P, 4], fp32)
            g_scaled = sb("g_scaled", [P, ST, D], fp32)
            relu_t = [sb(f"relu_t{i}", [P, CR], fp32) for i in range(2)]
            gen_adj = sb("gen_adj", [P, CH, P], i32)
            gen_adjf = sb("gen_adjf", [P, CH, P], fp32)
            gen_adj_t = sb("gen_adj_t", [P, CR], fp32)
            gen_feat = sb("gen_feat", [P, D], fp32)
            eps = sb("eps2", [P, 1], fp32)
            stats = sb("stats2", [P, CH, 6], fp32)
            moments = [sb(f"moments2_{i}", [P, CH, 2], fp32) for i in range(2)]
            std = [sb(f"std2_{i}", [P, CH], fp32) for i in range(2)]
            rstd = [sb(f"rstd2_{i}", [P, CH], fp32) for i in range(2)]
            shift = [sb(f"shift2_{i}", [P, CH], fp32) for i in range(2)]
            assert HK == 2

            def general_sums(name, evacuate):
                block_in = sem(f"gen_in_{name}")
                converted = sem(f"gen_converted_{name}")
                block_turned = sem(f"gen_turned_{name}")
                block_copied = sem(f"gen_copied_{name}")
                multiplied = sem(f"gen_multiplied_{name}")
                summed = sem(f"gen_summed_{name}")
                gen_own = sem(f"gen_own_{name}")

                def general_sync(sync):
                    with sync.Fori(0, NC) as c:
                        with sync.Fori(0, NT) as jb:
                            sync.wait_ge(multiplied, c * NT + jb)
                            stand_apart(sync)
                            sync.dma_start(gen_adj[:, :, :], adj[bass.ds(c * CR, CR), bass.ds(jb * P, P)].rearrange("(s p) j -> p s j", p=P)).then_inc(block_in, 16)

                def general_vector(dve):
                    v = Chain(dve, gen_own)
                    with dve.Fori(0, NC) as c:
                        with dve.Fori(0, NT) as jb:
                            dve.wait_ge(block_in, (c * NT + jb) * 16 + 16)
                            v(nc.vector.tensor_scalar(gen_adjf[:, :, :], gen_adj[:, :, :], 2.0, None, ALU.mult))
                            v(nc.vector.tensor_tensor(gen_feat[:, :], feat_hi[:, bass.ds(jb, 1), :].rearrange("p o d -> p (o d)"),
                                                      feat_lo[:, bass.ds(jb, 1), :].rearrange("p o d -> p (o d)"), ALU.add))
                            v.restart()
                            dve.sem_inc(converted, 1)
                        dve.wait_ge(multiplied, c * NT + NT)
                        v(evacuate(dve, neigh_t[:, bass.ds(c * CR, CR)], bank[1][:, 0:CR]))
                        v.restart()
                        dve.sem_inc(summed, 1)

                def general_scalar(act):
                    with act.Fori(0, NC * NT) as n:
                        act.wait_ge(block_turned, n + 1)
                        nc.scalar.activation(gen_adj_t[:, :], bank[0][:, 0:CR], ACT.Copy).then_inc(block_copied, 1)

                def general_tensor(pe):
                    with pe.Fori(0, NC) as c:
                        def block_of(jb, first, final):
                            pe.wait_ge(converted, c * NT + jb + 1)
                            for s in range(CH):
                                last = nc.tensor.transpose(bank[0][:, s * P:(s + 1) * P], gen_adjf[:, s, :], ident[:, :])
                            last.then_inc(block_turned, 1)
                            pe.wait_ge(block_copied, c * NT + jb + 1)
                            if first:
                                pe.wait_ge(summed, c)
                            nc.tensor.matmul(bank[1][:, 0:CR], gen_feat[:, :], gen_adj_t[:, :], start=first, stop=final).then_inc(multiplied, 1)
                        block_of(0, True, False)
                        with pe.Fori(1, NT - 1) as jb:
                            block_of(jb, False, False)
                        block_of(NT - 1, False, True)

                with nc.Block() as block:
                    @block.sync
                    def _(sync):
                        with sync.If(general(sync) != 0):
                            general_sync(sync)
                        with sync.Else():
                            sync.nop()

                    @block.tensor
                    def _(pe):
                        with pe.If(general(pe) != 0):
                            general_tensor(pe)
                        with pe.Else():
                            pe.nop()

                    @block.scalar
                    def _(act):
                        with act.If(general(act) != 0):
                            general_scalar(act)
                        with act.Else():
                            act.nop()

                    @block.vector
                    def _(dve):
                        with dve.If(general(dve) != 0):
                            general_vector(dve)
                        with dve.Else():
                            dve.nop()

            general_sums("a", take_neighbour_sum)

            w_landed = sem("w_landed")
            w_turned = sem("w_turned")
            w_ready = sem("w_ready")
            x1_landed = [sem(f"x1_landed{i}") for i in range(2)]
            x1_turned = sem("x1_turned")
            x1t_ready = sem("x1t_ready")
            hid_sum = sem("hid_sum")
            hid_ready = sem("hid_ready")
            g_sum = sem("g_sum")
            g_ready = sem("g_ready")
            self_sum = sem("self_sum")
            self_ready = sem("self_ready")
            g_own = sem("g_own")
            gm_ready = sem("gm_ready")
            gm_all = sem("gm_all")
            split_own = sem("split_own")
            g32 = [feat_hi[:, :, :].bitcast(fp32), feat_lo[:, :, :].bitcast(fp32)]

            with nc.Block() as block:
                @block.sync
                def _(sync):
                    for n, w in enumerate((w_self_0, w_neigh_0)):
                        sync.dma_start(w_raw[:, n * HK:(n + 1) * HK, :], w.rearrange("(k p) d -> p k d", p=P)).then_inc(w_landed, 16)
                    for n, w in enumerate((w_self_1, w_neigh_1)):
                        sync.dma_start(w_raw[:, (n + 2) * HK:(n + 3) * HK, :], w.rearrange("o (k d) -> o k d", d=P)).then_inc(w_landed, 16)

                    def load(c, par, skip):
                        if not skip:
                            sync.wait_ge(x1_turned, c - 1)
                        sync.dma_start(x1c[par][:, :, :], x1_dram[bass.ds(c * CR, CR), :].rearrange("(s p) d -> p s d", p=P)).then_inc(x1_landed[par], 16)
                    load(0, 0, True)
                    load(1, 1, True)
                    with sync.Fori(1, NC // 2) as pair:
                        c = pair * 2
                        load(c, 0, False)
                        load(c + 1, 1, False)

                @block.tensor
                def _(pe):
                    pe.wait_ge(w_landed, 64)
                    for n in range(4 * HK):
                        last = nc.tensor.transpose(bank[n // 4][:, (n % 4) * P:(n % 4 + 1) * P], w_raw[:, n, :], ident[:, :])
                    last.then_inc(w_turned, 1)
                    pe.wait_ge(w_ready, 2)

                    def chunk(c, par, skip):
                        pe.wait_ge(x1_landed[par], c // 2 * 16 + 16)
                        if not skip:
                            pe.wait_ge(x1t_ready, c)
                        for s in range(CH):
                            last = nc.tensor.transpose(bank[0][:, s * P:(s + 1) * P], x1c[par][:, s, :], ident[:, :])
                        last.then_inc(x1_turned, 1)
                        pe.wait_ge(x1t_ready, c + 1)
                        for hh in range(HK):
                            if not skip:
                                pe.wait_ge(hid_ready, c * HK - HK + hh + 1)
                            nc.tensor.matmul(bank[1 + hh][:, 0:CR], w_t[:, hh, :], x1t[par][:, :], start=True, stop=False)
                            nc.tensor.matmul(bank[1 + hh][:, 0:CR], w_t[:, HK + hh, :], neigh_t[:, bass.ds(c * CR, CR)], start=False, stop=True).then_inc(hid_sum, 1)
                        pe.wait_ge(hid_ready, c * HK + HK)
                        if not skip:
                            pe.wait_ge(g_ready, c)
                            pe.wait_ge(self_ready, c)
                        for s in range(CH):
                            for kk in range(HK):
                                last = nc.tensor.matmul(bank[3][:, s * P:(s + 1) * P], hid[par][:, kk, s * P:(s + 1) * P], w_t[:, 3 * HK + kk, :],
                                                        start=(kk == 0), stop=(kk == HK - 1))
                        last.then_inc(g_sum, 1)
                        for kk in range(HK):
                            last = nc.tensor.matmul(bank[4][:, 0:CR], w_t[:, 2 * HK + kk, :], hid[par][:, kk, :], start=(kk == 0), stop=(kk == HK - 1))
                        last.then_inc(self_sum, 1)
                    chunk(0, 0, True)
                    chunk(1, 1, False)
                    with pe.Fori(1, NC // 2) as pair:
                        c = pair * 2
                        chunk(c, 0, False)
                        chunk(c + 1, 1, False)

                @block.scalar
                def _(act):
                    def chunk(c, par, skip):
                        act.wait_ge(x1_turned, c + 1)
                        nc.scalar.activation(x1t[par][:, :], bank[0][:, 0:CR], ACT.Copy).then_inc(x1t_ready, 1)
                        for hh in range(HK):
                            act.wait_ge(hid_sum, c * HK + hh + 1)
                            if not skip:
                                act.wait_ge(self_sum, c - 1)
                            nc.scalar.activation(hid[par][:, hh, :], bank[1 + hh][:, 0:CR], ACT.Relu).then_inc(hid_ready, 1)
                    chunk(0, 0, True)
                    chunk(1, 1, True)
                    with act.Fori(1, NC // 2) as pair:
                        c = pair * 2
                        chunk(c, 0, False)
                        chunk(c + 1, 1, False)

                @block.gpsimd
                def _(pool):
                    pool.wait_ge(gm_ready, 1)
                    pool.partition_all_reduce(gm[:, 1:2], gm[:, 0:1], P, bass.bass_isa.ReduceOp.max).then_inc(gm_all, 1)

                @block.vector
                def _(dve):
                    v = Chain(dve, g_own)
                    dve.wait_ge(w_turned, 1)
                    for n in range(2):
                        nc.vector.tensor_copy(w_t[:, 4 * n:4 * n + 4, :].rearrange("p a b -> p (a b)"), bank[n][:, :]).then_inc(w_ready, 1)

                    def chunk(c):
                        dve.wait_ge(g_sum, c + 1)
                        parts = bank[3][:, :].rearrange("p (s h d) -> p s h d", s=CH, h=2)
                        for hf in range(2):
                            nc.vector.tensor_copy(g32[hf][:, bass.ds(c * CH, CH), :], parts[:, :, hf, :])
                        nc.vector.tensor_reduce(gmax[:, bass.ds(c, 1)], bank[3][:, :], AX.X, ALU.max, apply_absolute_value=True).then_inc(g_ready, 1)
                        dve.wait_ge(self_sum, c + 1)
                        nc.vector.tensor_copy(neigh_t[:, bass.ds(c * CR, CR)], bank[4][:, 0:CR]).then_inc(self_ready, 1)
                    with dve.Fori(0, NC) as c:
                        chunk(c)
                    dve.wait_ge(g_ready, NC)
                    v(nc.vector.tensor_reduce(gm[:, 0:1], gmax[:, :], AX.X, ALU.max))
                    v.wait()
                    v(nc.vector.tensor_scalar(gm[:, 0:1], gm[:, 0:1], 2.0 ** -100, None, ALU.max))
                    v.wait()
                    dve.sem_inc(gm_ready, 1)
                    dve.wait_ge(gm_all, 1)
                    v(nc.vector.tensor_scalar(gm[:, 1:2].bitcast(u32), gm[:, 1:2].bitcast(u32), 0x7F800000, None, ALU.bitwise_and))
                    v.wait()
                    v(nc.vector.tensor_scalar(gm[:, 3:4], gm[:, 1:2], 2.0 ** -15, None, ALU.mult))
                    v(nc.vector.reciprocal(gm[:, 2:3], gm[:, 1:2]))
                    v.wait()
                    v(nc.vector.tensor_scalar(gm[:, 2:3], gm[:, 2:3], 2.0 ** 14, None, ALU.mult))
                    v.wait()
                    v.restart()

            def add_self_term(eng, rows, sums):
                return nc.vector.scalar_tensor_tensor(rows, sums, gm[:, 3:4], rows, ALU.mult, ALU.add)

            with nc.Block() as block:
                @block.vector
                def _(dve):
                    v = Chain(dve, split_own)

                    def split(u):
                        of_group = bass.ds(u * ST, ST)
                        for hf in range(2):
                            v(nc.vector.tensor_scalar(g_scaled[:, :, hf * (D // 2):(hf + 1) * (D // 2)], g32[hf][:, of_group, :], gm[:, 2:3], None, ALU.mult))
                        v.wait()
                        v(nc.vector.tensor_copy(feat_hi[:, of_group, :], g_scaled[:, :, :]))
                        v.wait()
                        v(nc.vector.tensor_tensor(feat_lo[:, of_group, :], g_scaled[:, :, :], feat_hi[:, of_group, :], ALU.subtract))
                        v.restart()
                        dve.sem_inc(feat_ready["b"], 1)
                    with dve.If(general(dve) == 0):
                        split(0)
                        open_blocks(dve, "b", 0, 0, ST)
                        with dve.Fori(1, NG) as u:
                            split(u)
                            for k in range(ST):
                                open_block(dve, "b", 0, u * ST + k, k % 2)
                        take_sums(dve, "b", 0, add_self_term)
                        open_blocks(dve, "b", 1, 0, NT)
                        take_sums(dve, "b", 1, add_self_term)
                        dve.wait_ge(sums_read_v["b"], 2 * BANKS)
                    with dve.Else():
                        with dve.Fori(0, NG) as u:
                            split(u)

                @block.tensor
                def _(pe):
                    with pe.If(general(pe) == 0):
                        for half in range(2):
                            multiply_half(pe, "b", half)
                    with pe.Else():
                        pe.nop()
            general_sums("b", add_self_term)

            res_landed = [sem(f"res_landed{i}") for i in range(2)]
            relu_ready = sem("relu_ready")
            turned = sem("turned")
            residual_added = sem("residual_added")
            var2_ready = sem("var2_ready")
            std2_ready = sem("std2_ready")
            fin_own = sem("fin_own")
            scales_ready = sem("scales_ready")
            out_ready = sem("out_ready")
            YB = 4
            NQ = NC // YB
            y = [hid[i // 2][:, i % 2, :].rearrange("p (s d) -> p s d", d=D) for i in range(YB)]
            out_stored = [sem(f"out_stored{i}") for i in range(YB)]
            def rows_of_chunk(t, c):
                return t[bass.ds(c * CR, CR), :].rearrange("(s p) d -> p s d", p=P)

            with nc.Block() as block:
                @block.sync
                def _(sync):
                    def load(c, par, skip):
                        if not skip:
                            sync.wait_ge(residual_added, c - 1)
                        sync.dma_start(x1c[par][:, :, :], rows_of_chunk(x1_dram, c)).then_inc(res_landed[par], 16)
                    load(0, 0, True)
                    load(1, 1, True)
                    with sync.Fori(1, NC // 2) as pair:
                        c = pair * 2
                        load(c, 0, False)
                        load(c + 1, 1, False)

                @block.gpsimd
                def _(pool):
                    def store(q):
                        for i in range(YB):
                            pool.wait_ge(out_ready, q * YB + i + 1)
                            stand_apart(pool)
                            pool.dma_start(rows_of_chunk(out, q * YB + i), y[i]).then_inc(out_stored[i], 16)
                    with pool.Fori(0, NC // YB) as q:
                        store(q)
                    for i in range(YB):
                        pool.wait_ge(out_stored[i], NC // YB * 16)

                @block.tensor
                def _(pe):
                    def chunk(c, par, skip):
                        pe.wait_ge(relu_ready, c + 1)
                        if not skip:
                            pe.wait_ge(residual_added, c - 1)
                        for s in range(CH):
                            last = nc.tensor.transpose(bank[par][:, s * P:(s + 1) * P], relu_t[par][:, s * P:(s + 1) * P], ident[:, :])
                        last.then_inc(turned, 1)
                    chunk(0, 0, True)
                    chunk(1, 1, True)
                    with pe.Fori(1, NC // 2) as pair:
                        c = pair * 2
                        chunk(c, 0, False)
                        chunk(c + 1, 1, False)

                @block.scalar
                def _(act):
                    def relu(c, par, skip):
                        if not skip:
                            act.wait_ge(turned, c - 1)
                        nc.scalar.activation(relu_t[par][:, :], neigh_t[:, bass.ds(c * CR, CR)], ACT.Relu).then_inc(relu_ready, 1)

                    def root(c, i):
                        act.wait_ge(var2_ready, c + 1)
                        nc.scalar.activation(std[i % 2][:, :], moments[i % 2][:, :, 1], ACT.Sqrt, bias=eps[:, :]).then_inc(std2_ready, 1)

                    def scale_rows(c, i):
                        act.wait_ge(scales_ready, c + 1)
                        for s in range(CH):
                            last = nc.scalar.activation(y[i][:, s, :], y[i][:, s, :], ACT.Identity,
                                                        scale=rstd[i % 2][:, s:s + 1], bias=shift[i % 2][:, s:s + 1])
                        last.then_inc(out_ready, 1)

                    def chunks(q, first, final):
                        for i in range(YB):
                            c = q * YB + i
                            if not (final and i == YB - 1):
                                relu(c + 1, (i + 1) % 2, first and i == 0)
                            root(c, i)
                            if not (first and i == 0):
                                scale_rows(c - 1, (i - 1) % YB)
                    relu(0, 0, True)
                    chunks(0, True, NQ == 1)
                    if NQ > 2:
                        with act.Fori(1, NQ - 1) as q:
                            chunks(q, False, False)
                    if NQ > 1:
                        chunks(NQ - 1, False, True)
                    scale_rows(NC - 1, YB - 1)

                @block.vector
                def _(dve):
                    v = Chain(dve, fin_own)
                    v(nc.vector.memset(eps[:, :], EPS))
                    v.restart()

                    def take_moments(c, i, skip):
                        dve.wait_ge(turned, c + 1)
                        dve.wait_ge(res_landed[i % 2], c // 2 * 16 + 16)
                        if not skip:
                            dve.wait_ge(out_stored[i], c // YB * 16)
                        v(nc.vector.tensor_tensor(y[i].rearrange("p s d -> p (s d)"), bank[i % 2][:, 0:CR],
                                                  x1c[i % 2][:, :, :].rearrange("p s d -> p (s d)"), ALU.add))
                        v.wait()
                        dve.sem_inc(residual_added, 1)
                        for s in range(CH):
                            v(nc.vector.bn_stats(stats[:, s, :], y[i][:, s, :]))
                        v.wait()
                        for s in range(CH):
                            v(nc.vector.bn_aggr(moments[i % 2][:, s, :], stats[:, s, :]))
                        v.wait()
                        dve.sem_inc(var2_ready, 1)

                    def take_scales(c, i):
                        dve.wait_ge(std2_ready, c + 1)
                        v(nc.vector.reciprocal(rstd[i % 2][:, :], std[i % 2][:, :]))
                        v.wait()
                        v(nc.vector.scalar_tensor_tensor(shift[i % 2][:, :], moments[i % 2][:, :, 0], -1.0, rstd[i % 2][:, :], ALU.mult, ALU.mult))
                        v.wait()
                        dve.sem_inc(scales_ready, 1)

                    def chunks(q, first):
                        for i in range(YB):
                            take_moments(q * YB + i, i, first)
                            if not (first and i == 0):
                                take_scales(q * YB + i - 1, (i - 1) % YB)
                        v.restart()
                    chunks(0, True)
                    if NQ > 1:
                        with dve.Fori(1, NQ) as q:
                            chunks(q, False)
                    take_scales(NC - 1, YB - 1)


def kernel(x, adj, L1_gnn_w_self_0, L1_gnn_w_neigh_0, L1_gnn_w_self_1, L1_gnn_w_neigh_1):
    import numpy as _np
    import concourse.bacc as _bacc
    from concourse.bass_utils import run_bass_kernel_spmd as _run

    given = {
        "x": x, "adj": adj, "w_self_0": L1_gnn_w_self_0, "w_neigh_0": L1_gnn_w_neigh_0,
        "w_self_1": L1_gnn_w_self_1, "w_neigh_1": L1_gnn_w_neigh_1,
    }
    nc = _bacc.Bacc("TRN2", target_bir_lowering=False, num_devices=1)
    arrays, args = {}, []
    for name, a in given.items():
        a = _np.ascontiguousarray(a)
        arrays[f"in_{name}"] = a
        args.append(nc.dram_tensor(f"in_{name}", a.shape, mybir.dt.from_np(a.dtype), kind="ExternalInput").ap())
    out = nc.dram_tensor("out_0", arrays["in_x"].shape, mybir.dt.float32, kind="ExternalOutput").ap()
    graph_max_then_sum_layers(nc, *args, out)
    r = _run(nc, [arrays], core_ids=[0])
    return r.results[0]["out_0"]
```

```python
import concourse.bass as bass
from concourse import mybir
from contextlib import ExitStack


def graph_max_then_sum_layers(nc, x, adj, w_self_0, w_neigh_0, w_self_1, w_neigh_1, out):
    fp32 = mybir.dt.float32
    bf16 = mybir.dt.bfloat16
    fp16 = mybir.dt.float16
    fp8 = mybir.dt.float8e4
    i32 = mybir.dt.int32
    u32 = mybir.dt.uint32
    u16 = mybir.dt.uint16
    ALU = mybir.AluOpType
    ACT = mybir.ActivationFunctionType
    AX = mybir.AxisListType

    N, D = x.shape
    P = 128
    H = w_self_0.shape[0]
    HK = H // P
    NT = N // P
    ST = 8
    NG = NT // ST
    GR = ST * P
    WB = 16
    NW = N // WB
    WT = P // WB
    GB = NG // 4
    GS = GB * GR
    NWS = (N - GS) // WB
    TOP = 24
    LEVELS = 3
    LC = 32
    C_DEG, C_ROW = 24, 25
    CAPS = [24, 12, 11, 10, 9, 8, 7, 6]
    G_AT = [0, 24, 0, 12, 24, 0, 12, 24]
    REDUCED = [-1, 0, 1, 1, 2, 3, 4, 5]
    MB = 4
    LATE = 5
    EPS = 1e-5
    FP8_ONE = 9
    DEG_BIAS = -7.0 / 16.0
    DEG_BASE = N * DEG_BIAS * DEG_BIAS
    X_SCALE = 4096.0
    NEGATIVE = -3.4028234663852886e38
    DEG_PARTS = 8
    DP = N // DEG_PARTS

    list_dram = nc.dram_tensor("neighbour_lists", (N, LC), u32, kind="Internal").ap()
    max_dram = nc.dram_tensor("neighbour_max", (N, D), fp32, kind="Internal").ap()
    x1_dram = nc.dram_tensor("layer0_out", (N + 1, D), fp32, kind="Internal").ap()
    g_dram = nc.dram_tensor("hidden_product", (N + 1, D), fp32, kind="Internal").ap()
    sum_dram = nc.dram_tensor("neighbour_sums", (GS, D), fp32, kind="Internal").ap()

    def group_rows(t, u):
        return t[bass.ds(u * GR, GR), :].rearrange("(s p) d -> p s d", p=P)

    class Chain:

        def __init__(self, eng, sem):
            self.eng, self.sem, self.n = eng, sem, 0

        def __call__(self, ins):
            ins.then_inc(self.sem, 1)
            self.n += 1
            return self.n

        def wait(self, n=None):
            if self.n:
                self.eng.wait_ge(self.sem, self.n if n is None else n)

        def restart(self):
            if self.n:
                self.wait()
                self.eng.sem_clear(self.sem)
            self.n = 0

    def after(eng, sem, value):
        if not isinstance(value, int) or value > 0:
            eng.wait_ge(sem, value)

    with ExitStack() as whole:
        def allocator(stack):
            def sb(name, shape, dt):
                return stack.enter_context(nc.sbuf_tensor("sb_" + name, shape, dt))

            def pb(name, shape, dt):
                return stack.enter_context(nc.psum_tensor("ps_" + name, shape, dt))

            def sem(name):
                return stack.enter_context(nc.semaphore(name))
            return sb, pb, sem

        sb, pb, sem = allocator(whole)
        adj_t_bits = sb("adj_t_bits", [P, NT, NWS], u16)
        feat_hi = sb("feat_hi", [P, NT, D], fp16)
        feat_lo = sb("feat_lo", [P, NT, D], fp16)
        ident = sb("ident", [P, P], fp32)
        adj_rows = [sb(f"adj_rows{i}", [P, N], i32) for i in range(2)]
        HN = (N - GS) // 2
        HWD = NWS // 2
        BANKS = 8
        OB = 2
        BPB = WB // BANKS
        CH = 4
        CR = CH * P
        NC = NT // CH
        neigh_t = adj_rows[0][:, :].bitcast(fp32)
        open_bits = [adj_rows[1][:, :].bitcast(u16)[:, i * 2 * WB * HWD:(i + 1) * 2 * WB * HWD].rearrange("p (o b w) -> p o b w", o=2, b=WB) for i in range(OB)]
        bank = [pb(f"bank{i}", [P, 512], fp32) for i in range(BANKS)]
        gathered = sb("gathered", [P, 36, D], fp32)
        near_max = [sb(f"near_max{i}", [P, D], fp32) for i in range(MB)]
        sum_lists = sb("sum_lists", [P, ST, LC], u32)
        sum_at = sb("sum_at", [P, ST, TOP], u32)
        spare_slots = sb("spare_slots", [P, ST, TOP], fp32)
        slot_number = sb("slot_number", [P, TOP], i32)
        sum_nat = [sb(f"sum_nat{i}", [P, ST, D], fp32) for i in range(2)]
        zero_row = sb("zero_row", [1, D], fp32)
        flag = sb("flag", [P, 1], fp32)
        flag_all = sb("flag_all", [P, 1], fp32)
        flag_word = sb("flag_word", [P, 1], i32)

        waits = {e: sem(f"waits_{n}") for n, e in enumerate((nc.tensor.engine, nc.scalar.engine, nc.gpsimd.engine, nc.vector.engine, nc.sync.engine))}

        def stand_apart(eng):
            eng.sem_inc(waits[eng.engine], 1)

        opened, opened_used, sums_ready, sums_read_v, sums_read_a, feat_ready = (
            {layer: sem(f"{name}_{layer}") for layer in "ab"}
            for name in ("opened", "opened_used", "sums_ready", "sums_read_v", "sums_read_a", "feat_ready"))

        PARTS = {"a": ((0, 0, NG - 1), (1, 0, NG), (0, NG - 1, NG)), "b": ((0, 0, NG), (1, 0, NG))}
        GP = ST // 2

        def pairs_before(layer, part):
            return sum((g1 - g0) * GP for _, g0, g1 in PARTS[layer][:part])

        def open_pair(dve, layer, part, q, buf):
            half, g0, _ = PARTS[layer][part]
            place, before = q - g0 * GP, pairs_before(layer, part)
            if not isinstance(q, int) or place >= OB:
                dve.wait_ge(opened_used[layer], before - part + place - OB + 1)
            elif part and place == OB - 1:
                dve.wait_ge(sums_ready[layer], part * BANKS)
            elif part:
                dve.wait_ge(opened_used[layer], before - part - (OB - place - 2))
            for b in range(WB):
                shift = (14 - b, ALU.logical_shift_left) if b <= 14 else (1, ALU.logical_shift_right)
                last = nc.vector.tensor_scalar(open_bits[buf][:, :, b, :], adj_t_bits[:, bass.ds(q * 2, 2), half * HWD:(half + 1) * HWD],
                                               shift[0], 0x4000, shift[1], ALU.bitwise_and)
            last.then_inc(opened[layer], 1)

        def open_blocks(dve, layer, part, start, end):
            q, end, first = start // 2, end // 2, PARTS[layer][part][1] * GP
            while q < end:
                rounds = (end - q) // OB
                if q - first >= OB and q % OB == 0 and rounds > 1:
                    with dve.Fori(q // OB, q // OB + rounds) as n:
                        for buf in range(OB):
                            open_pair(dve, layer, part, n * OB + buf, buf)
                    q += rounds * OB
                else:
                    open_pair(dve, layer, part, q, q % OB)
                    q += 1

        def multiply_part(pe, layer, part):
            _, g0, g1 = PARTS[layer][part]

            def multiply(q, odd, buf, first, final):
                if not odd:
                    pe.wait_ge(opened[layer], pairs_before(layer, part) + q - g0 * GP + 1)
                jb = q * 2 + odd
                for n, feat in enumerate((feat_hi, feat_lo)):
                    for g in range(BANKS):
                        if first and n == 0 and part:
                            if layer == "a" and g % 2:
                                pe.wait_ge(sums_read_a[layer], (part - 1) * (BANKS // 2) + g // 2 + 1)
                            elif layer == "a":
                                pe.wait_ge(sums_read_v[layer], (part - 1) * (BANKS // 2) + g // 2 + 1)
                            else:
                                pe.wait_ge(sums_read_v[layer], (part - 1) * BANKS + g + 1)
                        last = nc.tensor.matmul(
                            bank[g][:, 0:BPB * HWD], feat[:, bass.ds(jb, 1), :].rearrange("p o d -> p (o d)"),
                            open_bits[buf][:, odd, BPB * g:BPB * (g + 1), :].bitcast(fp16).rearrange("p b w -> p (b w)"),
                            start=(first and n == 0), stop=(final and n == 1))
                        if final and n == 1:
                            last.then_inc(sums_ready[layer], 1)
                if odd and not final:
                    last.then_inc(opened_used[layer], 1)

            def group(u, first, final):
                pe.wait_ge(feat_ready[layer], u + 1)
                for k in range(ST):
                    multiply(u * GP + k // 2, k % 2, k // 2 % OB, first and k == 0, final and k == ST - 1)
            group(g0, True, g1 - g0 == 1)
            if g1 - g0 > 2:
                with pe.Fori(g0 + 1, g1 - 1) as u:
                    group(u, False, False)
            if g1 - g0 > 1:
                group(g1 - 1, False, True)

        def rows_of(half, g):
            part = neigh_t[:, GS + half * HN:GS + (half + 1) * HN].rearrange("p (w b) -> p b w", b=WB)
            return part[:, BPB * g:BPB * (g + 1), :]

        def bank_rows(g):
            return bank[g][:, 0:BPB * HWD].rearrange("p (b w) -> p b w", b=BPB)

        def take_sums(eng, layer, part, evacuate, shared=False):
            on_act = eng.engine == nc.scalar.engine
            for g in range(int(on_act), BANKS, 2 if shared else 1):
                eng.wait_ge(sums_ready[layer], part * BANKS + g + 1)
                evacuate(eng, rows_of(PARTS[layer][part][0], g), bank_rows(g)).then_inc((sums_read_a if on_act else sums_read_v)[layer], 1)

        def take_neighbour_sum(eng, rows, sums):
            if eng.engine == nc.scalar.engine:
                return nc.scalar.activation(rows, sums, ACT.Copy, scale=0.5 / X_SCALE)
            return nc.vector.tensor_scalar(rows, sums, 0.5 / X_SCALE, None, ALU.mult)

        def add_neighbour_sum(eng, rows, sums):
            return nc.vector.scalar_tensor_tensor(rows, sums, 0.5 / X_SCALE, rows, ALU.mult, ALU.add)

        sum_lists_in, sum_at_ready, sums_reduced, sum_nat_in, sums_turned, sums_taken, zero_stored = (
            sem(name) for name in ("sum_lists_in", "sum_at_ready", "sums_reduced", "sum_nat_in", "sums_turned", "sums_taken", "zero_stored"))
        sum_landed = [sem(f"sum_landed{s}") for s in range(ST)]
        sum_stored = [sem(f"sum_stored{i}") for i in range(MB)]

        def gather_sums(pool, rnd, g, table):
            def store_sum(s):
                pool.wait_ge(sums_reduced, rnd * ST + s + 1)
                pool.indirect_dma_start(sum_dram, bass.IndirectOffsetOnAxis(ap=sum_lists[:, s, C_ROW:C_ROW + 1], axis=0),
                                        near_max[s % MB][:, :], None, bounds_check=GS - 1, oob_is_err=False).then_inc(sum_stored[s % MB], 16)
            pool.dma_start(sum_lists[:, :, :], group_rows(list_dram, g)).then_inc(sum_lists_in, 16)
            pool.wait_ge(sum_at_ready, rnd + 1)
            for s in range(ST):
                if rnd * ST + REDUCED[s] > 0:
                    pool.wait_ge(sums_reduced, rnd * ST + REDUCED[s])
                for k in range(CAPS[s]):
                    pool.indirect_dma_start(gathered[:, G_AT[s] + k, :], None, table,
                                            bass.IndirectOffsetOnAxis(ap=sum_at[:, s, k:k + 1], axis=0),
                                            bounds_check=N, oob_is_err=False).then_inc(sum_landed[s], 16)
                if s >= 2:
                    store_sum(s - 2)
            store_sum(ST - 2)
            store_sum(ST - 1)
            for i in range(MB):
                pool.wait_ge(sum_stored[i], (rnd + 1) * (ST // MB) * 16)
            if rnd >= 2:
                pool.wait_ge(sums_turned, (rnd - 1) * 2)
            pool.dma_start(sum_nat[rnd % 2][:, :, :], group_rows(sum_dram, g)).then_inc(sum_nat_in, 16)

        def place_slots(dve, v, rnd):
            dve.wait_ge(sum_lists_in, (rnd + 1) * 16)
            v(nc.vector.tensor_tensor(spare_slots[:, :, :], slot_number[:, :].unsqueeze(1).to_broadcast([P, ST, TOP]),
                                      sum_lists[:, :, C_DEG:C_DEG + 1].to_broadcast([P, ST, TOP]), ALU.is_ge))
            v.wait()
            v(nc.vector.scalar_tensor_tensor(sum_at[:, :, :], spare_slots[:, :, :], float(N), sum_lists[:, :, 0:TOP], ALU.mult, ALU.max))
            v.wait()
            dve.sem_inc(sum_at_ready, 1)

        def reduce_sum(dve, v, rnd, s):
            dve.wait_ge(sum_landed[s], (rnd + 1) * CAPS[s] * 16)
            if rnd * (ST // MB) + s // MB:
                dve.wait_ge(sum_stored[s % MB], (rnd * (ST // MB) + s // MB) * 16)
            v(nc.vector.tensor_reduce(near_max[s % MB][:, :], gathered[:, G_AT[s]:G_AT[s] + CAPS[s], :].rearrange("p k d -> p d k"), AX.X, ALU.add))
            v.wait()
            dve.sem_inc(sums_reduced, 1)

        def turned_sums(rnd, half):
            return bank[4 + rnd % 2 * 2 + half][:, 0:GR // 2]

        def turn_sums(pe, rnd):
            pe.wait_ge(sum_nat_in, (rnd + 1) * 16)
            for half in range(2):
                for s in range(ST // 2):
                    last = nc.tensor.transpose(turned_sums(rnd, half)[:, s * P:(s + 1) * P], sum_nat[rnd % 2][:, half * ST // 2 + s, :], ident[:, :])
                last.then_inc(sums_turned, 1)

        def take_turned_sums(dve, v, rnd, g, take):
            for half in range(2):
                dve.wait_ge(sums_turned, rnd * 2 + half + 1)
                take(neigh_t[:, g * GR + half * GR // 2:g * GR + (half + 1) * GR // 2], turned_sums(rnd, half))
                v.wait()
                dve.sem_inc(sums_taken, 1)

        with ExitStack() as stage:
            sb, pb, sem = allocator(stage)
            ones = sb("ones", [P, P], fp32)
            pow2 = sb("pow2", [P, WB], fp32)
            row_pack = sb("row_pack", [P, WB, P], bf16)
            col_terms = sb("col_terms", [P, WT, WB], fp32)
            col_sum = sb("col_sum", [P, WT], fp32)
            col_pack = sb("col_pack", [P, WT], bf16)
            deg_bias = sb("deg_bias", [P, 1], fp32)
            eps = sb("eps", [P, 1], fp32)
            caps = sb("caps", [P, ST], fp32)
            local_row = sb("local_row", [P, ST], i32)
            local_rowf = sb("local_rowf", [P, ST], fp32)
            global_row = sb("global_row", [P, ST], fp32)
            word = sb("word", [P, ST, TOP], fp32)
            word_at = sb("word_at", [P, ST, TOP], u32)
            base = sb("base", [P, ST, TOP], fp32)
            bit = sb("bit", [P, ST, LEVELS, TOP], fp32)
            cand = sb("cand", [P, ST, LEVELS, TOP], fp32)
            near = sb("near", [P, ST, TOP], fp32)
            near_on = sb("near_on", [P, ST, TOP], fp32)
            deg_parts = sb("deg_parts", [P, ST, DEG_PARTS], fp32)
            deg = sb("deg", [P, ST], fp32)
            listed = sb("listed", [P, ST], fp32)
            key = sb("key", [P, ST], fp32)
            key_diag = sb("key_diag", [P, ST // 2, P], fp32)
            rest = key_diag[:, :, :].rearrange("p s q -> p (s q)")[:, 0:NW]
            rank_junk = sb("rank_junk", [P, GR], mybir.dt.uint8)
            rank = sb("rank", [P, ST], fp32)
            rank_u = sb("rank_u", [P, ST], u32)
            record = sb("record", [P, ST, LC], u32)
            lists = [sb(f"lists{i}", [P, ST, LC], u32) for i in range(2)]
            degrees = sb("degrees", [P, ST], u32)
            has_near = sb("has_near", [P, ST], fp32)
            over = sb("over", [P, ST], fp32)
            over1 = sb("over1", [P, 1], fp32)
            x_nat = [f[:, NT - ST:NT, :].bitcast(fp32).rearrange("p s (h d) -> p (s h d)", h=1).rearrange("p (s d) -> p s d", d=D)
                     for f in (feat_hi, feat_lo)]
            m_nat = sb("m_nat", [P, ST, D], fp32)
            stats = sb("stats", [P, ST, 6], fp32)
            moments = sb("moments", [P, ST, 2], fp32)
            std = sb("std", [P, ST], fp32)
            rstd = sb("rstd", [P, ST], fp32)
            WORD_BANKS = 4
            NORM_AT = 4
            KEYS_AT = 2
            pw = [bank[i][:, 0:NW] for i in range(WORD_BANKS)]
            pt = [bank[4 + i][:, 0:NT * WT] for i in range(2)]
            pk = [bank[6 + i][:, 0:GR // 2] for i in range(2)]

            deg_junk = [sb(f"deg_junk{i}", [P, DP], fp8) for i in range(2)]

            adj_landed = [sem(f"adj_landed{i}") for i in range(2)]
            const_a = sem("const_a")
            const_v = sem("const_v")
            words_ready = sem("words_ready")
            words_read = sem("words_read")
            words_t_ready = sem("words_t_ready")
            words_t_read = sem("words_t_read")
            deg_ready = sem("deg_ready")
            deg_read = sem("deg_read")
            diag_ready = sem("diag_ready")
            keys_ready = sem("keys_ready")
            keys_read = sem("keys_read")
            vec = sem("vec")
            act_own = sem("act_own")
            pool_own = sem("pool_own")
            records_ready = sem("records_ready")
            records_stored = sem("records_stored")
            lists_landed = sem("lists_landed")
            gather_landed = [sem(f"gather_landed{s}") for s in range(ST)]
            degrees_copied = sem("degrees_copied")
            max_ready = sem("max_ready")
            max_stored = [sem(f"max_stored{i}") for i in range(MB)]
            nat_landed = sem("nat_landed")
            var_ready = sem("var_ready")
            std_ready = sem("std_ready")
            x1_ready = sem("x1_ready")
            x1_stored = sem("x1_stored")
            block = stage.enter_context(nc.Block())

            @block.sync
            def _(sync):
                def group(u):
                    for t in range(ST):
                        after(sync, words_t_ready, u * ST + t - 1)
                        after(sync, deg_ready, u * ST + t - 1)
                        sync.dma_start(adj_rows[t % 2][:, :], adj[bass.ds((u * ST + t) * P, P), :]).then_inc(adj_landed[t % 2], 16)
                group(0)
                if NG > 1:
                    with sync.Fori(1, NG) as u:
                        group(u)

            @block.tensor
            def _(pe):
                pe.wait_ge(const_v, 1)

                def keys(u):
                    for half in range(2):
                        pe.wait_ge(diag_ready, u * 2 + half + 1)
                        nc.tensor.matmul(pk[half], ones[:, :], key_diag[:, :, :].rearrange("p s q -> p (s q)"), start=True, stop=True).then_inc(keys_ready, 1)

                def group(u, sorted_group):
                    for t in range(ST):
                        if t == KEYS_AT and sorted_group is not None:
                            keys(sorted_group)
                        by_byte = adj_rows[t % 2][:, :].bitcast(fp8)
                        by_word = by_byte.rearrange("p (c k b) -> p c k b", k=WB, b=4)
                        by_block = by_byte.rearrange("p (j q b) -> p j q b", q=P, b=4)
                        pe.wait_ge(adj_landed[t % 2], (u * (ST // 2) + t // 2 + 1) * 16)
                        after(pe, words_read, u * ST + t - WORD_BANKS + 1)
                        stand_apart(pe)
                        for k in range(WB):
                            last = nc.tensor.matmul(pw[t % WORD_BANKS], row_pack[:, k, :], by_word[:, :, k, 0], start=(k == 0), stop=(k == WB - 1))
                        last.then_inc(words_ready, 1)
                        after(pe, words_t_read, u * ST + t - 1)
                        stand_apart(pe)
                        for j in range(NT):
                            last = nc.tensor.matmul(pt[t % 2][:, j * WT:(j + 1) * WT], by_block[:, j, :, 0], col_pack[:, :], start=True, stop=True)
                        last.then_inc(words_t_ready, 1)
                group(0, None)
                if NG > 1:
                    with pe.Fori(1, NG) as u:
                        group(u, u - 1)
                keys(NG - 1)
                pe.wait_ge(words_t_read, NT)
                pe.wait_ge(records_ready, NG)
                for part in range(3):
                    multiply_part(pe, "a", part)
                if GB:
                    pe.wait_ge(sums_read_v["a"], 2 * BANKS)
                    pe.wait_ge(sums_read_a["a"], BANKS)
                    turn_sums(pe, 0)

            @block.scalar
            def _(act):
                a = Chain(act, act_own)
                act.wait_ge(const_a, 1)

                def root(norm):
                    act.wait_ge(var_ready, norm + 1)
                    nc.scalar.activation(std[:, :], moments[:, :, 1], ACT.Sqrt, bias=eps[:, :]).then_inc(std_ready, 1)

                def group(u, norm):
                    for t in range(ST):
                        act.wait_ge(adj_landed[t % 2], (u * (ST // 2) + t // 2 + 1) * 16)
                        if t == 0:
                            after(act, deg_read, u)
                        stand_apart(act)
                        for c in range(DEG_PARTS):
                            if a.n >= 2:
                                a.wait(a.n - 1)
                            a(nc.scalar.activation(deg_junk[c % 2][:, :], adj_rows[t % 2][:, c * DP:(c + 1) * DP], ACT.Square,
                                                   bias=deg_bias[:, :], accum_out=deg_parts[:, t, c:c + 1], saturate=False))
                        a.wait()
                        act.sem_inc(deg_ready, 1)
                        act.wait_ge(words_t_ready, u * ST + t + 1)
                        at = (u * ST + t) * WT - (0 if isinstance(u, int) and u < GB else NW - NWS)
                        nc.scalar.activation(adj_t_bits[:, :, bass.ds(at, WT)],
                                             pt[t % 2].rearrange("p (j w) -> p j w", w=WT), ACT.Copy).then_inc(words_t_read, 1)
                        if t == NORM_AT and norm is not None:
                            root(norm)
                    a.restart()
                for u in range(min(3, NG)):
                    group(u, None)
                if NG > 3:
                    with act.Fori(3, NG) as u:
                        group(u, u - 3)
                for norm in range(max(0, NG - 3), NG - 1):
                    root(norm)
                take_sums(act, "a", 0, take_neighbour_sum, shared=True)
                root(NG - 1)
                take_sums(act, "a", 1, take_neighbour_sum, shared=True)

            @block.gpsimd
            def _(pool):
                pool.memset(ident[:, :], 0.0).then_inc(pool_own, 1)
                pool.wait_ge(pool_own, 1)
                pool.affine_select(out=ident[:, :], in_=ident[:, :], compare_op=ALU.not_equal, fill=1.0, base=0,
                                   pattern=[[-1, P]], channel_multiplier=1).then_inc(pool_own, 1)
                pool.memset(ones[:, :], 1.0).then_inc(pool_own, 1)
                for k in range(WB):
                    pool.memset(pow2[:, k:k + 1], 2.0 ** (k + FP8_ONE)).then_inc(pool_own, 1)
                for s in range(ST):
                    pool.memset(caps[:, s:s + 1], float(CAPS[s])).then_inc(pool_own, 1)
                pool.memset(deg_bias[:, :], DEG_BIAS).then_inc(pool_own, 1)
                pool.memset(eps[:, :], EPS).then_inc(pool_own, 1)
                pool.iota(local_row[:, :], [[P, ST]], channel_multiplier=1).then_inc(pool_own, 1)
                pool.memset(flag[:, :], 0.0).then_inc(pool_own, 1)
                pool.iota(slot_number[:, :], [[1, TOP]], channel_multiplier=0).then_inc(pool_own, 1)
                pool.memset(zero_row[:, :], 0.0).then_inc(pool_own, 1)
                done = 2 + 1 + WB + ST + 6
                pool.wait_ge(pool_own, done)
                pool.sem_inc(const_a, 1)

                def store_lists(u):
                    pool.wait_ge(records_ready, u + 1)
                    stand_apart(pool)
                    for t in range(ST):
                        pool.indirect_dma_start(list_dram, bass.IndirectOffsetOnAxis(ap=rank_u[:, t:t + 1], axis=0),
                                                record[:, t, :], None, bounds_check=N - 1, oob_is_err=False).then_inc(records_stored, 16)

                def load_natural(u):
                    for i in range(MB):
                        pool.wait_ge(max_stored[i], (u + 1) * (ST // MB) * 16)
                        stand_apart(pool)
                    after(pool, x1_stored, u * 16)
                    stand_apart(pool)
                    pool.dma_start(m_nat[:, :, :], group_rows(max_dram, u)).then_inc(nat_landed, 16)
                    for half in range(2):
                        pool.dma_start(x_nat[half], group_rows(x, u)[:, half * ST // 2:(half + 1) * ST // 2, :]).then_inc(nat_landed, 16)

                def store_x1(u):
                    pool.wait_ge(x1_ready, u + 1)
                    stand_apart(pool)
                    pool.dma_start(group_rows(x1_dram, u), m_nat[:, :, :]).then_inc(x1_stored, 16)

                def store_max(u, s, par):
                    pool.wait_ge(max_ready, u * ST + s + 1)
                    stand_apart(pool)
                    pool.indirect_dma_start(max_dram, bass.IndirectOffsetOnAxis(ap=lists[par][:, s, C_ROW:C_ROW + 1], axis=0),
                                            near_max[s % MB][:, :], None, bounds_check=N - 1, oob_is_err=False).then_inc(max_stored[s % MB], 16)

                def load_lists(u, par):
                    pool.wait_ge(records_stored, (u + 1) * ST * 16)
                    stand_apart(pool)
                    if not isinstance(u, int) or u > 1:
                        for i in range(MB):
                            pool.wait_ge(max_stored[i], (u - 1) * (ST // MB) * 16)
                            stand_apart(pool)
                    pool.dma_start(lists[par][:, :, :], group_rows(list_dram, u)).then_inc(lists_landed, 16)

                def copy_degrees(u, par):
                    pool.wait_ge(lists_landed, (u + 1) * 16)
                    stand_apart(pool)
                    after(pool, max_ready, u * ST - ST + 1)
                    stand_apart(pool)
                    pool.tensor_copy(degrees[:, :], lists[par][:, :, C_DEG]).then_inc(degrees_copied, 1)
                    pool.wait_ge(degrees_copied, u + 1)
                    stand_apart(pool)

                def gather(u, s, par):
                    after(pool, max_ready, u * ST + REDUCED[s])
                    stand_apart(pool)
                    for k in range(CAPS[s]):
                        pool.indirect_dma_start(gathered[:, G_AT[s] + k, :], None, x,
                                                bass.IndirectOffsetOnAxis(ap=lists[par][:, s, k:k + 1], axis=0),
                                                bounds_check=N - 1, oob_is_err=False).then_inc(gather_landed[s], 16)

                def group(u, par, before, stored, following):
                    for s in range(ST):
                        if s == LATE and following:
                            store_lists(u + 1)
                        gather(u, s, par)
                        if s < 2:
                            if before is not None:
                                store_max(before, ST - 2 + s, 1 - par)
                        else:
                            store_max(u, s - 2, par)
                        if s == 0 and stored is not None:
                            store_x1(stored)
                        if s == 2 and before is not None:
                            load_natural(before)
                        if s == LATE and following:
                            load_lists(u + 1, 1 - par)
                    if following:
                        copy_degrees(u + 1, 1 - par)

                for t in (x1_dram, g_dram):
                    pool.dma_start(t[N:N + 1, :], zero_row[:, :]).then_inc(zero_stored, 16)
                store_lists(0)
                load_lists(0, 0)
                copy_degrees(0, 0)
                group(0, 0, None, None, True)
                if NG > 2:
                    group(1, 1, 0, None, True)
                    if NG > 4:
                        with pool.Fori(1, NG // 2 - 1) as pair:
                            for par in range(2):
                                u = pair * 2 + par
                                group(u, par, u - 1, u - 2, True)
                    group(NG - 2, 0, NG - 3, NG - 4, True)
                group(NG - 1, 1, NG - 2, NG - 3 if NG > 2 else None, False)
                for s in range(ST - 2, ST):
                    store_max(NG - 1, s, 1)
                store_x1(NG - 2)
                load_natural(NG - 1)
                store_x1(NG - 1)
                pool.wait_ge(x1_stored, NG * 16)
                pool.wait_ge(zero_stored, 32)
                if GB:
                    gather_sums(pool, 0, 0, x1_dram)

            @block.vector
            def _(dve):
                v = Chain(dve, vec)
                TT, TS, STT = nc.vector.tensor_tensor, nc.vector.tensor_scalar, nc.vector.scalar_tensor_tensor
                dve.wait_ge(const_a, 1)
                v(TT(row_pack[:, :, :], ident[:, :].unsqueeze(1).to_broadcast([P, WB, P]),
                     pow2[:, :].unsqueeze(2).to_broadcast([P, WB, P]), ALU.mult))
                v(TT(col_terms[:, :, :], ident[:, :].rearrange("p (m k) -> p m k", k=WB),
                     pow2[:, :].unsqueeze(1).to_broadcast([P, WT, WB]), ALU.mult))
                v(nc.vector.tensor_copy(local_rowf[:, :], local_row[:, :]))
                v(nc.vector.tensor_copy(global_row[:, :], local_row[:, :]))
                v(nc.vector.memset(record[:, :, :].bitcast(fp32), 0.0))
                v.wait()
                v(nc.vector.tensor_reduce(col_sum[:, :], col_terms[:, :, :], AX.X, ALU.add))
                v.wait()
                v(nc.vector.tensor_copy(col_pack[:, :], col_sum[:, :]))
                v.wait()
                dve.sem_inc(const_v, 1)

                def extract(u, t):
                    dve.wait_ge(words_ready, u * ST + t + 1)
                    stand_apart(dve)
                    source = pw[t % WORD_BANKS]
                    for r in range(TOP // 8):
                        eight = word[:, t, 8 * r:8 * r + 8]
                        v(nc.vector.max(eight, source))
                        v.wait()
                        v(nc.vector.max_index(word_at[:, t, 8 * r:8 * r + 8], eight, source))
                        if r < TOP // 8 - 1:
                            v(nc.vector.match_replace(rest, eight, source, 0.0))
                            source = rest
                            if r == 0:
                                v.wait()
                                dve.sem_inc(words_read, 1)
                        v.wait()

                def neighbours(u):
                    dve.wait_ge(deg_ready, (u + 1) * ST)
                    v(nc.vector.tensor_reduce(deg[:, :], deg_parts[:, :, :], AX.X, ALU.add))
                    v.wait()
                    dve.sem_inc(deg_read, 1)
                    b = [bit[:, :, lv, :] for lv in range(LEVELS)]
                    left = word[:, :, :]
                    v(TS(base[:, :, :], word_at[:, :, :], float(WB), float(1 - 127), ALU.mult, ALU.add))
                    for lv in range(LEVELS):
                        v(TS(b[lv].bitcast(u32), left.bitcast(u32), 0x7F800000, None, ALU.bitwise_and))
                        v.wait()
                        if lv < LEVELS - 1:
                            v(TT(left, left, b[lv], ALU.subtract))
                            v.wait()
                    v(TS(cand[:, :, :, :].bitcast(u32), bit[:, :, :, :].bitcast(u32), 23, None, ALU.logical_shift_right))
                    v.wait()
                    v(TT(cand[:, :, :, :], cand[:, :, :, :].bitcast(u32), base[:, :, :].unsqueeze(2).to_broadcast([P, ST, LEVELS, TOP]), ALU.add))
                    v.wait()
                    v(STT(cand[:, :, :, :], bit[:, :, :, :], 0.0, cand[:, :, :, :], ALU.is_gt, ALU.mult))
                    v.wait()
                    for r in range(TOP // 8):
                        for t in range(ST):
                            v(nc.vector.max(near[:, t, 8 * r:8 * r + 8], cand[:, t, :, :].rearrange("p l k -> p (l k)")))
                        v.wait()
                        if r < TOP // 8 - 1:
                            for t in range(ST):
                                flat = cand[:, t, :, :].rearrange("p l k -> p (l k)")
                                v(nc.vector.match_replace(flat, near[:, t, 8 * r:8 * r + 8], flat, 0.0))
                            v.wait()
                    v(TS(near_on[:, :, :], near[:, :, :], 0.0, None, ALU.is_gt))
                    v(TS(deg[:, :], deg[:, :], -DEG_BASE, 8.0, ALU.add, ALU.mult))
                    v.wait()
                    v(nc.vector.tensor_reduce(listed[:, :], near_on[:, :, :], AX.X, ALU.add))
                    v.wait()
                    v(TT(over[:, :], deg[:, :], listed[:, :], ALU.not_equal))
                    v(TS(key[:, :], deg[:, :], 64.0, float(GR), ALU.min, ALU.mult))
                    v.wait()
                    v(nc.vector.tensor_reduce(over1[:, :], over[:, :], AX.X, ALU.max))
                    v(TT(key[:, :], key[:, :], local_rowf[:, :], ALU.add))
                    v.wait()
                    v(TT(flag[:, :], flag[:, :], over1[:, :], ALU.max))

                def sort_rows(u):
                    for half in range(2):
                        if half:
                            dve.wait_ge(keys_ready, u * 2 + 1)
                        n = ST // 2
                        v(TT(key_diag[:, :, :], ident[:, :].unsqueeze(1).to_broadcast([P, n, P]),
                             key[:, half * n:half * n + n].unsqueeze(2).to_broadcast([P, n, P]), ALU.mult))
                        v.wait()
                        dve.sem_inc(diag_ready, 1)
                    v(TS(near_on[:, :, :], near_on[:, :, :], -1.0, 1.0, ALU.mult, ALU.add))
                    v.wait()
                    v(TT(near_on[:, :, :], near_on[:, :, :], near[:, :, 0:1].to_broadcast([P, ST, TOP]), ALU.mult))
                    v.wait()
                    v(TT(near[:, :, :], near[:, :, :], near_on[:, :, :], ALU.add))
                    after(dve, records_stored, u * ST * 16)
                    v.wait()
                    v(TS(near[:, :, :], near[:, :, :], 1.0, float(N), ALU.max, ALU.min))
                    v.wait()
                    v(TS(record[:, :, 0:TOP], near[:, :, :], -1.0, None, ALU.add))
                    v(TS(record[:, :, C_DEG], deg[:, :], 64.0, None, ALU.min))
                    v(nc.vector.tensor_copy(record[:, :, C_ROW], global_row[:, :]))
                    for half in range(2):
                        dve.wait_ge(keys_ready, u * 2 + half + 1)
                    for t in range(ST):
                        for half in range(2):
                            v(TS(rank_junk[:, half * GR // 2:(half + 1) * GR // 2], pk[half], key[:, t:t + 1],
                                 0.0 if half == 0 else rank[:, t:t + 1], ALU.is_gt, ALU.add, accum_out=rank[:, t:t + 1]))
                            if half == 0:
                                v.wait()
                    v.wait()
                    v(TT(rank[:, :], rank[:, :], global_row[:, :], ALU.add))
                    v.wait()
                    v(TT(rank_u[:, :], rank[:, :], local_rowf[:, :], ALU.subtract))
                    v.wait()
                    v(TS(global_row[:, :], global_row[:, :], float(GR), None, ALU.add))
                    dve.sem_inc(records_ready, 1)

                def reduce_max(u, s):
                    dve.wait_ge(gather_landed[s], (u + 1) * CAPS[s] * 16)
                    if s == 0:
                        v(TS(has_near[:, :], degrees[:, :], 0.0, None, ALU.is_gt))
                        v(TT(over[:, :], degrees[:, :], caps[:, :], ALU.is_gt))
                        v.wait()
                        v(nc.vector.tensor_reduce(over1[:, :], over[:, :], AX.X, ALU.max))
                        v.wait()
                        v(TT(flag[:, :], flag[:, :], over1[:, :], ALU.max))
                    after(dve, max_stored[s % MB], (u * (ST // MB) + s // MB) * 16)
                    v(nc.vector.tensor_reduce(near_max[s % MB][:, :], gathered[:, G_AT[s]:G_AT[s] + CAPS[s], :].rearrange("p k d -> p d k"), AX.X, ALU.max))
                    v.wait()
                    v(TS(near_max[s % MB][:, :], near_max[s % MB][:, :], has_near[:, s:s + 1], None, ALU.mult))
                    v.wait()
                    dve.sem_inc(max_ready, 1)

                def take_moments(u):
                    dve.wait_ge(nat_landed, (u + 1) * 48)
                    for half in range(2):
                        part = m_nat[:, half * ST // 2:(half + 1) * ST // 2, :]
                        v(TT(part, part, x_nat[half], ALU.add))
                    v.wait()
                    for s in range(ST):
                        v(nc.vector.bn_stats(stats[:, s, :], m_nat[:, s, :]))
                    v.wait()
                    for s in range(ST):
                        v(nc.vector.bn_aggr(moments[:, s, :], stats[:, s, :]))
                    v.wait()
                    dve.sem_inc(var_ready, 1)

                def scale_rows(u):
                    dve.wait_ge(std_ready, u + 1)
                    v(nc.vector.reciprocal(rstd[:, :], std[:, :]))
                    v.wait()
                    for s in range(ST):
                        v(TS(m_nat[:, s, :], m_nat[:, s, :], moments[:, s, 0:1], rstd[:, s:s + 1], ALU.subtract, ALU.mult))
                    v.wait()
                    dve.sem_inc(x1_ready, 1)
                    hi = feat_hi[:, bass.ds(u * ST, ST), :]
                    v(TS(hi, m_nat[:, :, :], X_SCALE, None, ALU.mult))
                    v.wait()
                    v(STT(feat_lo[:, bass.ds(u * ST, ST), :], m_nat[:, :, :], X_SCALE, hi, ALU.mult, ALU.subtract))
                    v.wait()
                    dve.sem_inc(feat_ready["a"], 1)

                def normalise(u):
                    take_moments(u)
                    scale_rows(u)

                def group(u, late, reduced, normed):
                    turns = {1: ((late, 3),), 2: ((late, 4),), 5: ((late, 5),), 6: ((late, 6),), 7: ((late, 7),)}

                    def reduce_if(g, s):
                        if g is not None:
                            reduce_max(g, s)
                    for t in range(ST):
                        extract(u, t)
                        if t == NORM_AT - 2 and normed is not None:
                            take_moments(normed)
                        if t == NORM_AT - 1 and normed is not None:
                            scale_rows(normed)
                        for turn in turns.get(t, ()):
                            reduce_if(*turn)
                    neighbours(u)
                    reduce_if(reduced, 0)
                    sort_rows(u)
                    reduce_if(reduced, 1)
                    reduce_if(reduced, 2)
                    v.restart()

                v.restart()
                group(0, None, None, None)
                group(1, None, 0, None)
                if NG > 2:
                    group(2, 0, 1, None)
                if NG > 3:
                    with dve.Fori(3, NG) as u:
                        group(u, u - 2, u - 1, u - 3)

                LAST, BEFORE = NG - 1, NG - 2
                dve.wait_ge(words_t_read, NT)
                dve.wait_ge(words_t_ready, NT)
                dve.wait_ge(deg_ready, NT)
                LAST, BEFORE = NG - 1, NG - 2
                def open_between(part, steps, behind):
                    at, end = 2 * min(part, 1), PARTS["a"][part][2] * ST
                    for n, (place, what, *of) in enumerate(steps):
                        if what is normalise and of[0] < 0:
                            continue
                        place = min([place, behind] + [g[0] * ST for _, w, *g in steps[n:] if w is normalise])
                        open_blocks(dve, "a", part, at, max(at, min(place, end)))
                        at = max(at, min(place, end))
                        what(*of)
                    open_blocks(dve, "a", part, at, end)
                open_between(0, (
                    (4, normalise, NG - 3), (8, reduce_max, BEFORE, 3), (10, reduce_max, BEFORE, 4), (16, reduce_max, BEFORE, 5),
                    (20, reduce_max, BEFORE, 6), (22, reduce_max, BEFORE, 7), (32, reduce_max, LAST, 0), (38, reduce_max, LAST, 1),
                    (44, reduce_max, LAST, 2), (46, normalise, BEFORE), (48, reduce_max, LAST, 3), (54, reduce_max, LAST, 4)), NT)
                open_pair(dve, "a", 1, 0, 0)
                take_sums(dve, "a", 0, take_neighbour_sum, shared=True)
                gathered_steps = ((20, place_slots, dve, v, 0),) + tuple(
                    (place, reduce_sum, dve, v, 0, s) for s, place in enumerate((34, 38, 42, 46, 50, 54, 58, 60)))
                open_between(1, (
                    (4, reduce_max, LAST, 5), (6, reduce_max, LAST, 6), (10, reduce_max, LAST, 7), (18, normalise, LAST))
                    + (gathered_steps if GB else ()), NT)
                open_pair(dve, "a", 2, LAST * GP, 0)
                take_sums(dve, "a", 1, take_neighbour_sum, shared=True)
                open_blocks(dve, "a", 2, LAST * ST + 2, NT)
                take_sums(dve, "a", 2, add_neighbour_sum)
                if GB:
                    take_turned_sums(dve, v, 0, 0, lambda rows, sums: v(nc.vector.tensor_copy(rows, sums)))
                v.restart()

        sb, pb, sem = allocator(whole)
        w_raw = sb("w_raw", [P, 4 * HK, P], fp32)
        w_landed = sem("w_landed")
        flag_reduced = sem("flag_reduced")
        flag_own = sem("flag_own")
        with nc.Block() as block:
            @block.sync
            def _(sync):
                for n, w in enumerate((w_self_0, w_neigh_0)):
                    sync.dma_start(w_raw[:, n * HK:(n + 1) * HK, :], w.rearrange("(k p) d -> p k d", p=P)).then_inc(w_landed, 16)
                for n, w in enumerate((w_self_1, w_neigh_1)):
                    sync.dma_start(w_raw[:, (n + 2) * HK:(n + 3) * HK, :], w.rearrange("o (k d) -> o k d", d=P)).then_inc(w_landed, 16)

            @block.gpsimd
            def _(pool):
                pool.partition_all_reduce(flag_all[:, :], flag[:, :], P, bass.bass_isa.ReduceOp.max).then_inc(flag_reduced, 1)

            @block.vector
            def _(dve):
                dve.wait_ge(flag_reduced, 1)
                nc.vector.tensor_scalar(flag_all[:, :], flag_all[:, :], 0.0, None, ALU.is_gt).then_inc(flag_own, 1)
                dve.wait_ge(flag_own, 1)
                nc.vector.tensor_copy(flag_word[:, :], flag_all[:, :]).then_inc(flag_own, 1)
                dve.wait_ge(flag_own, 2)

        def general(eng):
            return eng.value_load(flag_word[0:1, 0:1], min_val=0, max_val=1)

        with ExitStack() as stage:
            sb, pb, sem = allocator(stage)
            x_t = adj_t_bits[:, :, :].bitcast(fp32).rearrange("p a b -> p (a b)")
            if NT * NWS // 2 < N + N // 2:
                x_t = sb("x_t", [P, N + N // 2], fp32)
            max_t = [x_t[:, N:N + N // 2], gathered[:, :, :].rearrange("p k d -> p (k d)")[:, 0:N // 2]]
            x_t = x_t[:, 0:N]
            adj_row = adj_rows[0]
            penalty = adj_rows[1][:, :].bitcast(fp32)
            row_max = sb("row_max", [P, 2], fp32)
            x_tile = sb("x_tile", [P, D], fp32)
            m_tile = sb("m_tile", [P, P], fp32)
            eps = sb("eps0", [P, 1], fp32)
            stats = sb("stats0", [P, 6], fp32)
            moments = sb("moments0", [P, 2], fp32)
            std = sb("std0", [P, 1], fp32)
            turn = bank[0][:, 0:P]
            x_in = sem("gen_x_in")
            x_turned = sem("gen_x_turned")
            x_kept = sem("gen_x_kept")
            row_in = sem("gen_row_in")
            row_done = sem("gen_row_done")
            x_back = sem("gen_x_back")
            m_copied = sem("gen_m_copied")
            m_turned = sem("gen_m_turned")
            var_ready = sem("gen_var_ready")
            std_ready = sem("gen_std_ready")
            x1_ready = sem("gen_x1_ready")
            x1_out = sem("gen_x1_out")
            own = sem("gen_own")

            def tile_rows(t, i):
                return t[bass.ds(i * P, P), :]

            with nc.Block() as block:
                @block.sync
                def _(sync):
                    with sync.If(general(sync) != 0):
                        with sync.Fori(0, NT) as t:
                            sync.wait_ge(x_turned, t)
                            stand_apart(sync)
                            sync.dma_start(x_tile[:, :], tile_rows(x, t)).then_inc(x_in, 16)
                        with sync.Fori(0, N) as i:
                            sync.wait_ge(row_done, i)
                            stand_apart(sync)
                            sync.dma_start(adj_row[:, :], adj[bass.ds(i, 1), :].partition_broadcast(P)).then_inc(row_in, 16)
                        with sync.Fori(0, NT) as t:
                            sync.wait_ge(x1_ready, t)
                            stand_apart(sync)
                            sync.wait_ge(x_turned, NT)
                            sync.dma_start(x_tile[:, :], tile_rows(x, t)).then_inc(x_back, 16)
                            sync.wait_ge(x1_ready, t + 1)
                            stand_apart(sync)
                            sync.dma_start(tile_rows(x1_dram, t), x_tile[:, :]).then_inc(x1_out, 16)
                            sync.wait_ge(x1_out, t * 16 + 16)
                            stand_apart(sync)
                    with sync.Else():
                        sync.nop()

                @block.tensor
                def _(pe):
                    with pe.If(general(pe) != 0):
                        with pe.Fori(0, NT) as t:
                            pe.wait_ge(x_in, t * 16 + 16)
                            pe.wait_ge(x_kept, t)
                            nc.tensor.transpose(turn, x_tile[:, :], ident[:, :]).then_inc(x_turned, 1)
                        pe.wait_ge(x_kept, NT)
                        with pe.Fori(0, NT) as t:
                            pe.wait_ge(m_copied, t + 1)
                            nc.tensor.transpose(turn, m_tile[:, :], ident[:, :]).then_inc(m_turned, 1)
                    with pe.Else():
                        pe.nop()

                @block.scalar
                def _(act):
                    with act.If(general(act) != 0):
                        with act.Fori(0, NT) as t:
                            act.wait_ge(x_turned, t + 1)
                            nc.scalar.activation(x_t[:, bass.ds(t * P, P)], turn, ACT.Copy).then_inc(x_kept, 1)
                        with act.Fori(0, NT) as t:
                            act.wait_ge(var_ready, t + 1)
                            nc.scalar.activation(std[:, :], moments[:, 1:2], ACT.Sqrt, bias=eps[:, :]).then_inc(std_ready, 1)
                    with act.Else():
                        act.nop()

                @block.vector
                def _(dve):
                    with dve.If(general(dve) != 0):
                        v = Chain(dve, own)
                        TS, TT = nc.vector.tensor_scalar, nc.vector.tensor_tensor
                        v(nc.vector.memset(eps[:, :], EPS))
                        dve.wait_ge(x_kept, NT)
                        v.restart()
                        def take_row(i, part):
                            dve.wait_ge(row_in, i * 16 + 16)
                            v(TS(penalty, adj_row[:, :], 0.0, NEGATIVE, ALU.is_equal, ALU.mult))
                            v.wait()
                            v(nc.vector.tensor_reduce(row_max[:, 0:1], penalty, AX.X, ALU.max))
                            v.wait()
                            v(TT(penalty, penalty, x_t, ALU.add))
                            v(TS(row_max[:, 0:1], row_max[:, 0:1], 0.0, None, ALU.is_equal))
                            v.wait()
                            v(nc.vector.tensor_reduce(row_max[:, 1:2], penalty, AX.X, ALU.max))
                            v.wait()
                            v(TT(max_t[part][:, bass.ds(i - part * (N // 2), 1)], row_max[:, 0:1], row_max[:, 1:2], ALU.mult))
                            v.restart()
                            dve.sem_inc(row_done, 1)

                        def finish_tile(t, part):
                            v(nc.vector.tensor_copy(m_tile[:, :], max_t[part][:, bass.ds(t * P - part * (N // 2), P)]))
                            v.wait()
                            dve.sem_inc(m_copied, 1)
                            dve.wait_ge(m_turned, t + 1)
                            dve.wait_ge(x_back, t * 16 + 16)
                            v(TT(x_tile[:, :], turn, x_tile[:, :], ALU.add))
                            v.wait()
                            v(nc.vector.bn_stats(stats[:, :], x_tile[:, :]))
                            v.wait()
                            v(nc.vector.bn_aggr(moments[:, :], stats[:, :]))
                            v.wait()
                            dve.sem_inc(var_ready, 1)
                            dve.wait_ge(std_ready, t + 1)
                            v(nc.vector.reciprocal(row_max[:, 0:1], std[:, :]))
                            v.wait()
                            v(TS(x_tile[:, :], x_tile[:, :], moments[:, 0:1], row_max[:, 0:1], ALU.subtract, ALU.mult))
                            v.wait()
                            hi = feat_hi[:, bass.ds(t, 1), :].rearrange("p o d -> p (o d)")
                            v(TS(hi, x_tile[:, :], X_SCALE, None, ALU.mult))
                            v.wait()
                            v(nc.vector.scalar_tensor_tensor(feat_lo[:, bass.ds(t, 1), :].rearrange("p o d -> p (o d)"),
                                                             x_tile[:, :], X_SCALE, hi, ALU.mult, ALU.subtract))
                            v.restart()
                            dve.sem_inc(x1_ready, 1)
                        for part in range(2):
                            with dve.Fori(part * (N // 2), (part + 1) * (N // 2)) as i:
                                take_row(i, part)
                        for part in range(2):
                            with dve.Fori(part * (NT // 2), (part + 1) * (NT // 2)) as t:
                                finish_tile(t, part)
                    with dve.Else():
                        dve.nop()

        with ExitStack() as stage:
            sb, pb, sem = allocator(stage)
            w_t = sb("w_t", [P, 4 * HK, P], fp32)
            x1c = [sb(f"x1c{i}", [P, CH, D], fp32) for i in range(2)]
            x1t = [sb(f"x1t{i}", [P, CR], fp32) for i in range(2)]
            hid = [sb(f"hid{i}", [P, HK, CR], fp32) for i in range(2)]
            gmax = sb("gmax", [P, NC], fp32)
            gm = sb("gm", [P, 4], fp32)
            keep = sb("keep", [P, 1], fp32)
            g_scaled = w_raw
            assert 4 * HK == ST
            relu_t = [sb(f"relu_t{i}", [P, CR], fp32) for i in range(2)]
            gen_adj = hid[0][:, 0, :].bitcast(i32).rearrange("p (s j) -> p s j", j=P)
            gen_adjf = hid[0][:, 1, :].rearrange("p (s j) -> p s j", j=P)
            gen_adj_t = hid[1][:, 0, :]
            gen_feat = hid[1][:, 1, 0:D]
            eps = sb("eps2", [P, 1], fp32)
            stats = sb("stats2", [P, CH, 6], fp32)
            moments = [sb(f"moments2_{i}", [P, CH, 2], fp32) for i in range(2)]
            std = [sb(f"std2_{i}", [P, CH], fp32) for i in range(2)]
            rstd = [sb(f"rstd2_{i}", [P, CH], fp32) for i in range(2)]
            shift = [sb(f"shift2_{i}", [P, CH], fp32) for i in range(2)]
            assert HK == 2

            def general_sums(name, evacuate):
                block_in = sem(f"gen_in_{name}")
                converted = sem(f"gen_converted_{name}")
                block_turned = sem(f"gen_turned_{name}")
                block_copied = sem(f"gen_copied_{name}")
                multiplied = sem(f"gen_multiplied_{name}")
                summed = sem(f"gen_summed_{name}")
                gen_own = sem(f"gen_own_{name}")

                def general_sync(sync):
                    with sync.Fori(0, NC) as c:
                        with sync.Fori(0, NT) as jb:
                            sync.wait_ge(multiplied, c * NT + jb)
                            stand_apart(sync)
                            sync.dma_start(gen_adj, adj[bass.ds(c * CR, CR), bass.ds(jb * P, P)].rearrange("(s p) j -> p s j", p=P)).then_inc(block_in, 16)

                def general_vector(dve):
                    v = Chain(dve, gen_own)
                    with dve.Fori(0, NC) as c:
                        with dve.Fori(0, NT) as jb:
                            dve.wait_ge(block_in, (c * NT + jb) * 16 + 16)
                            v(nc.vector.tensor_scalar(gen_adjf, gen_adj, 2.0, None, ALU.mult))
                            v(nc.vector.tensor_tensor(gen_feat, feat_hi[:, bass.ds(jb, 1), :].rearrange("p o d -> p (o d)"),
                                                      feat_lo[:, bass.ds(jb, 1), :].rearrange("p o d -> p (o d)"), ALU.add))
                            v.restart()
                            dve.sem_inc(converted, 1)
                        dve.wait_ge(multiplied, c * NT + NT)
                        v(evacuate(dve, neigh_t[:, bass.ds(c * CR, CR)], bank[1][:, 0:CR]))
                        v.restart()
                        dve.sem_inc(summed, 1)

                def general_scalar(act):
                    with act.Fori(0, NC * NT) as n:
                        act.wait_ge(block_turned, n + 1)
                        nc.scalar.activation(gen_adj_t, bank[0][:, 0:CR], ACT.Copy).then_inc(block_copied, 1)

                def general_tensor(pe):
                    with pe.Fori(0, NC) as c:
                        def block_of(jb, first, final):
                            pe.wait_ge(converted, c * NT + jb + 1)
                            for s in range(CH):
                                last = nc.tensor.transpose(bank[0][:, s * P:(s + 1) * P], gen_adjf[:, s, :], ident[:, :])
                            last.then_inc(block_turned, 1)
                            pe.wait_ge(block_copied, c * NT + jb + 1)
                            if first:
                                pe.wait_ge(summed, c)
                            nc.tensor.matmul(bank[1][:, 0:CR], gen_feat, gen_adj_t, start=first, stop=final).then_inc(multiplied, 1)
                        block_of(0, True, False)
                        with pe.Fori(1, NT - 1) as jb:
                            block_of(jb, False, False)
                        block_of(NT - 1, False, True)

                with nc.Block() as block:
                    @block.sync
                    def _(sync):
                        with sync.If(general(sync) != 0):
                            general_sync(sync)
                        with sync.Else():
                            sync.nop()

                    @block.tensor
                    def _(pe):
                        with pe.If(general(pe) != 0):
                            general_tensor(pe)
                        with pe.Else():
                            pe.nop()

                    @block.scalar
                    def _(act):
                        with act.If(general(act) != 0):
                            general_scalar(act)
                        with act.Else():
                            act.nop()

                    @block.vector
                    def _(dve):
                        with dve.If(general(dve) != 0):
                            general_vector(dve)
                        with dve.Else():
                            dve.nop()

            general_sums("a", take_neighbour_sum)

            def rows_of_chunk(t, c):
                return t[bass.ds(c * CR, CR), :].rearrange("(s p) d -> p s d", p=P)

            GC = GS // CR

            def chunk_at(p):
                return p + GC if p < NC - GC else p - (NC - GC)

            w_turned = sem("w_turned")
            w_ready = sem("w_ready")
            x1_landed = [sem(f"x1_landed{i}") for i in range(2)]
            x1_turned = sem("x1_turned")
            x1t_ready = sem("x1t_ready")
            hid_sum = sem("hid_sum")
            hid_ready = sem("hid_ready")
            g_sum = sem("g_sum")
            g_ready = sem("g_ready")
            self_sum = sem("self_sum")
            self_ready = sem("self_ready")
            g_own = sem("g_own")
            g_stored = sem("g_stored")
            gm_ready = sem("gm_ready")
            gm_all = sem("gm_all")
            split_own = sem("split_own")
            g32 = [feat_hi[:, :, :].bitcast(fp32), feat_lo[:, :, :].bitcast(fp32)]

            with nc.Block() as block:
                @block.sync
                def _(sync):
                    def load(p, c, par, skip):
                        if not skip:
                            sync.wait_ge(x1_turned, p - 1)
                        sync.dma_start(x1c[par][:, :, :], rows_of_chunk(x1_dram, c)).then_inc(x1_landed[par], 16)

                    def store_g(p, c):
                        sync.wait_ge(g_ready, p + 1)
                        for hf in range(2):
                            sync.dma_start(rows_of_chunk(g_dram, c)[:, :, hf * (D // 2):(hf + 1) * (D // 2)],
                                           g32[hf][:, bass.ds(c * CH, CH), :]).then_inc(g_stored, 16)
                    load(0, chunk_at(0), 0, True)
                    load(1, chunk_at(1), 1, True)
                    with sync.Fori(1, (NC - GC) // 2) as pair:
                        for par in range(2):
                            p = pair * 2 + par
                            load(p, p + GC, par, False)
                            store_g(p - 2, p - 2 + GC)
                    for p in range(NC - GC, NC + 2):
                        if p < NC:
                            load(p, chunk_at(p), p % 2, False)
                        store_g(p - 2, chunk_at(p - 2))
                    sync.wait_ge(g_stored, NC * 32)

                @block.tensor
                def _(pe):
                    pe.wait_ge(w_landed, 64)
                    for n in range(4 * HK):
                        last = nc.tensor.transpose(bank[n // 4][:, (n % 4) * P:(n % 4 + 1) * P], w_raw[:, n, :], ident[:, :])
                    last.then_inc(w_turned, 1)
                    pe.wait_ge(w_ready, 2)

                    def turn(p, par, skip):
                        pe.wait_ge(x1_landed[par], p // 2 * 16 + 16)
                        if not skip:
                            pe.wait_ge(x1t_ready, p)
                        for s in range(CH):
                            last = nc.tensor.transpose(bank[0][:, s * P:(s + 1) * P], x1c[par][:, s, :], ident[:, :])
                        last.then_inc(x1_turned, 1)

                    def chunk(p, c, par, skip, more=True):
                        pe.wait_ge(x1t_ready, p + 1)
                        for hh in range(HK):
                            if not skip:
                                pe.wait_ge(hid_ready, p * HK - HK + hh + 1)
                            nc.tensor.matmul(bank[1 + hh][:, 0:CR], w_t[:, hh, :], x1t[par][:, :], start=True, stop=False)
                            nc.tensor.matmul(bank[1 + hh][:, 0:CR], w_t[:, HK + hh, :], neigh_t[:, bass.ds(c * CR, CR)], start=False, stop=True).then_inc(hid_sum, 1)
                        if more:
                            turn(p + 1, 1 - par, False)
                        pe.wait_ge(hid_ready, p * HK + HK)
                        if not skip:
                            pe.wait_ge(g_ready, p)
                            pe.wait_ge(self_ready, p)
                        for s in range(CH):
                            for kk in range(HK):
                                last = nc.tensor.matmul(bank[3][:, s * P:(s + 1) * P], hid[par][:, kk, s * P:(s + 1) * P], w_t[:, 3 * HK + kk, :],
                                                        start=(kk == 0), stop=(kk == HK - 1))
                        last.then_inc(g_sum, 1)
                        for kk in range(HK):
                            last = nc.tensor.matmul(bank[4][:, 0:CR], w_t[:, 2 * HK + kk, :], hid[par][:, kk, :], start=(kk == 0), stop=(kk == HK - 1))
                        last.then_inc(self_sum, 1)
                    turn(0, 0, True)
                    chunk(0, chunk_at(0), 0, True)
                    chunk(1, chunk_at(1), 1, False)
                    with pe.Fori(1, (NC - GC) // 2) as pair:
                        for par in range(2):
                            p = pair * 2 + par
                            chunk(p, p + GC, par, False)
                    for p in range(NC - GC, NC):
                        if GB > 1 and chunk_at(p) == GR // CR:
                            turn_sums(pe, 1)
                            pe.wait_ge(sums_taken, 4)
                        chunk(p, chunk_at(p), p % 2, False, p < NC - 1)

                @block.scalar
                def _(act):
                    def copy_turned(p, par):
                        act.wait_ge(x1_turned, p + 1)
                        nc.scalar.activation(x1t[par][:, :], bank[0][:, 0:CR], ACT.Copy).then_inc(x1t_ready, 1)

                    def chunk(p, par, skip, more=True):
                        for hh in range(HK):
                            act.wait_ge(hid_sum, p * HK + hh + 1)
                            if not skip:
                                act.wait_ge(self_sum, p - 1)
                            nc.scalar.activation(hid[par][:, hh, :], bank[1 + hh][:, 0:CR], ACT.Relu).then_inc(hid_ready, 1)
                        if more:
                            copy_turned(p + 1, 1 - par)
                    copy_turned(0, 0)
                    chunk(0, 0, True)
                    chunk(1, 1, True)
                    with act.Fori(1, NC // 2 - 1) as pair:
                        for par in range(2):
                            chunk(pair * 2 + par, par, False)
                    chunk(NC - 2, 0, False)
                    chunk(NC - 1, 1, False, False)

                @block.gpsimd
                def _(pool):
                    if GB > 1:
                        gather_sums(pool, 1, 1, x1_dram)
                    pool.wait_ge(gm_ready, 1)
                    pool.partition_all_reduce(gm[:, 1:2], gm[:, 0:1], P, bass.bass_isa.ReduceOp.max).then_inc(gm_all, 1)

                @block.vector
                def _(dve):
                    v = Chain(dve, g_own)
                    dve.wait_ge(w_turned, 1)
                    for n in range(2):
                        nc.vector.tensor_copy(w_t[:, 4 * n:4 * n + 4, :].rearrange("p a b -> p (a b)"), bank[n][:, :]).then_inc(w_ready, 1)

                    def chunk(p, c):
                        dve.wait_ge(g_sum, p + 1)
                        parts = bank[3][:, :].rearrange("p (s h d) -> p s h d", s=CH, h=2)
                        for hf in range(2):
                            nc.vector.tensor_copy(g32[hf][:, bass.ds(c * CH, CH), :], parts[:, :, hf, :])
                        nc.vector.tensor_reduce(gmax[:, bass.ds(c, 1)], bank[3][:, :], AX.X, ALU.max, apply_absolute_value=True).then_inc(g_ready, 1)
                        dve.wait_ge(self_sum, p + 1)
                        nc.vector.tensor_copy(neigh_t[:, bass.ds(c * CR, CR)], bank[4][:, 0:CR]).then_inc(self_ready, 1)

                    def chunks(start, end):
                        if end - start > 2 and end <= NC - GC:
                            with dve.Fori(start, end) as p:
                                chunk(p, p + GC)
                        else:
                            for p in range(start, end):
                                chunk(p, chunk_at(p))

                    def keep_general(rows, sums):
                        v(nc.vector.tensor_scalar(relu_t[0][:, :], sums, keep[:, :], None, ALU.mult))
                        v.wait()
                        v(nc.vector.scalar_tensor_tensor(rows, rows, flag_all[:, :], relu_t[0][:, :], ALU.mult, ALU.add))
                    at = 0
                    if GB > 1:
                        v(nc.vector.tensor_scalar(keep[:, :], flag_all[:, :], -1.0, 1.0, ALU.mult, ALU.add))
                        place_slots(dve, v, 1)
                        for s, place in enumerate((3, 5, 6, 8, 9, 10, 11, 12)):
                            chunks(at, place)
                            at = place
                            reduce_sum(dve, v, 1, s)
                        second = NC - GC + GR // CR
                        chunks(at, second)
                        at = second
                        take_turned_sums(dve, v, 1, 1, keep_general)
                    chunks(at, NC)
                    dve.wait_ge(g_ready, NC)
                    v(nc.vector.tensor_reduce(gm[:, 0:1], gmax[:, :], AX.X, ALU.max))
                    v.wait()
                    v(nc.vector.tensor_scalar(gm[:, 0:1], gm[:, 0:1], 2.0 ** -100, None, ALU.max))
                    v.wait()
                    dve.sem_inc(gm_ready, 1)
                    open_pair(dve, "b", 0, 0, 0)
                    dve.wait_ge(gm_all, 1)
                    v(nc.vector.tensor_scalar(gm[:, 1:2].bitcast(u32), gm[:, 1:2].bitcast(u32), 0x7F800000, None, ALU.bitwise_and))
                    v.wait()
                    v(nc.vector.tensor_scalar(gm[:, 3:4], gm[:, 1:2], 2.0 ** -15, None, ALU.mult))
                    v(nc.vector.reciprocal(gm[:, 2:3], gm[:, 1:2]))
                    v.wait()
                    v(nc.vector.tensor_scalar(gm[:, 2:3], gm[:, 2:3], 2.0 ** 14, None, ALU.mult))
                    v.wait()
                    v.restart()

            def add_self_term(eng, rows, sums):
                return nc.vector.scalar_tensor_tensor(rows, sums, gm[:, 3:4], rows, ALU.mult, ALU.add)

            with nc.Block() as block:
                @block.gpsimd
                def _(pool):
                    with pool.If(general(pool) == 0):
                        for g in range(GB):
                            gather_sums(pool, GB + g, g, g_dram)
                    with pool.Else():
                        pool.nop()

                @block.vector
                def _(dve):
                    v = Chain(dve, split_own)

                    def split(u):
                        of_group = bass.ds(u * ST, ST)
                        for hf in range(2):
                            v(nc.vector.tensor_scalar(g_scaled[:, :, hf * (D // 2):(hf + 1) * (D // 2)], g32[hf][:, of_group, :], gm[:, 2:3], None, ALU.mult))
                        v.wait()
                        v(nc.vector.tensor_copy(feat_hi[:, of_group, :], g_scaled[:, :, :]))
                        v.wait()
                        v(nc.vector.tensor_tensor(feat_lo[:, of_group, :], g_scaled[:, :, :], feat_hi[:, of_group, :], ALU.subtract))
                        v.restart()
                        dve.sem_inc(feat_ready["b"], 1)
                    with dve.If(general(dve) == 0):
                        def groups(start, end):
                            if start == 0 < end:
                                split(0)
                                open_blocks(dve, "b", 0, 2, ST)
                                start = 1
                            if end > start:
                                with dve.Fori(start, end) as u:
                                    split(u)
                                    for k in range(ST // 2):
                                        open_pair(dve, "b", 0, u * (ST // 2) + k, k % OB)

                        steps = [(0, place_slots, GB)] + [(n, reduce_sum, GB, s) for s, n in enumerate((2, 3, 4, 5, 6, 6, 7, 7))]
                        if GB > 1:
                            steps.append((8, place_slots, GB + 1))
                        at = 0
                        for place, step, *of in steps if GB else ():
                            groups(at, max(at, min(place, NG)))
                            at = max(at, min(place, NG))
                            step(dve, v, *of)
                            v.restart()
                        groups(at, NG)
                        open_pair(dve, "b", 1, 0, 0)
                        take_sums(dve, "b", 0, add_self_term)
                        at = 2
                        for s, place in enumerate((14, 20, 24, 28, 32, 36, 40, 42)) if GB > 1 else ():
                            open_blocks(dve, "b", 1, at, place)
                            at = place
                            reduce_sum(dve, v, GB + 1, s)
                        open_blocks(dve, "b", 1, at, NT)
                        take_sums(dve, "b", 1, add_self_term)
                        dve.wait_ge(sums_read_v["b"], 2 * BANKS)
                        for g in range(GB):
                            take_turned_sums(dve, v, GB + g, g, lambda rows, sums: v(nc.vector.tensor_tensor(rows, rows, sums, ALU.add)))
                        v.restart()
                    with dve.Else():
                        with dve.Fori(0, NG) as u:
                            split(u)

                @block.tensor
                def _(pe):
                    with pe.If(general(pe) == 0):
                        for half in range(2):
                            multiply_part(pe, "b", half)
                        pe.wait_ge(sums_read_v["b"], 2 * BANKS)
                        for g in range(GB):
                            turn_sums(pe, GB + g)
                    with pe.Else():
                        pe.nop()
            general_sums("b", add_self_term)

            res_landed = [sem(f"res_landed{i}") for i in range(2)]
            relu_ready = sem("relu_ready")
            turned = sem("turned")
            residual_added = sem("residual_added")
            var2_ready = sem("var2_ready")
            std2_ready = sem("std2_ready")
            fin_own = sem("fin_own")
            scales_ready = sem("scales_ready")
            out_ready = sem("out_ready")
            YB = 4
            NQ = NC // YB
            y = [hid[i // 2][:, i % 2, :].rearrange("p (s d) -> p s d", d=D) for i in range(YB)]
            out_stored = [sem(f"out_stored{i}") for i in range(YB)]
            with nc.Block() as block:
                @block.sync
                def _(sync):
                    def load(c, par, skip):
                        if not skip:
                            sync.wait_ge(residual_added, c - 1)
                        sync.dma_start(x1c[par][:, :, :], rows_of_chunk(x1_dram, c)).then_inc(res_landed[par], 16)
                    load(0, 0, True)
                    load(1, 1, True)
                    with sync.Fori(1, NC // 2) as pair:
                        c = pair * 2
                        load(c, 0, False)
                        load(c + 1, 1, False)

                @block.gpsimd
                def _(pool):
                    def store(q):
                        for i in range(YB):
                            pool.wait_ge(out_ready, q * YB + i + 1)
                            stand_apart(pool)
                            pool.dma_start(rows_of_chunk(out, q * YB + i), y[i]).then_inc(out_stored[i], 16)
                    with pool.Fori(0, NC // YB) as q:
                        store(q)
                    for i in range(YB):
                        pool.wait_ge(out_stored[i], NC // YB * 16)

                @block.tensor
                def _(pe):
                    def chunk(c, par, skip):
                        pe.wait_ge(relu_ready, c + 1)
                        if not skip:
                            pe.wait_ge(residual_added, c - 1)
                        for s in range(CH):
                            last = nc.tensor.transpose(bank[par][:, s * P:(s + 1) * P], relu_t[par][:, s * P:(s + 1) * P], ident[:, :])
                        last.then_inc(turned, 1)
                    chunk(0, 0, True)
                    chunk(1, 1, True)
                    with pe.Fori(1, NC // 2) as pair:
                        c = pair * 2
                        chunk(c, 0, False)
                        chunk(c + 1, 1, False)

                @block.scalar
                def _(act):
                    def relu(c, par, skip):
                        if not skip:
                            act.wait_ge(turned, c - 1)
                        nc.scalar.activation(relu_t[par][:, :], neigh_t[:, bass.ds(c * CR, CR)], ACT.Relu).then_inc(relu_ready, 1)

                    def root(c, i):
                        act.wait_ge(var2_ready, c + 1)
                        nc.scalar.activation(std[i % 2][:, :], moments[i % 2][:, :, 1], ACT.Sqrt, bias=eps[:, :]).then_inc(std2_ready, 1)

                    def scale_rows(c, i):
                        act.wait_ge(scales_ready, c + 1)
                        for s in range(CH):
                            last = nc.scalar.activation(y[i][:, s, :], y[i][:, s, :], ACT.Identity,
                                                        scale=rstd[i % 2][:, s:s + 1], bias=shift[i % 2][:, s:s + 1])
                        last.then_inc(out_ready, 1)

                    def chunks(q, first, final):
                        for i in range(YB):
                            c = q * YB + i
                            if not (final and i == YB - 1):
                                relu(c + 1, (i + 1) % 2, first and i == 0)
                            root(c, i)
                            if not (first and i == 0):
                                scale_rows(c - 1, (i - 1) % YB)
                    relu(0, 0, True)
                    chunks(0, True, NQ == 1)
                    if NQ > 2:
                        with act.Fori(1, NQ - 1) as q:
                            chunks(q, False, False)
                    if NQ > 1:
                        chunks(NQ - 1, False, True)
                    scale_rows(NC - 1, YB - 1)

                @block.vector
                def _(dve):
                    v = Chain(dve, fin_own)
                    v(nc.vector.memset(eps[:, :], EPS))
                    v.restart()

                    def take_moments(c, i, skip):
                        dve.wait_ge(turned, c + 1)
                        dve.wait_ge(res_landed[i % 2], c // 2 * 16 + 16)
                        if not skip:
                            dve.wait_ge(out_stored[i], c // YB * 16)
                        v(nc.vector.tensor_tensor(y[i].rearrange("p s d -> p (s d)"), bank[i % 2][:, 0:CR],
                                                  x1c[i % 2][:, :, :].rearrange("p s d -> p (s d)"), ALU.add))
                        v.wait()
                        dve.sem_inc(residual_added, 1)
                        for s in range(CH):
                            v(nc.vector.bn_stats(stats[:, s, :], y[i][:, s, :]))
                        v.wait()
                        for s in range(CH):
                            v(nc.vector.bn_aggr(moments[i % 2][:, s, :], stats[:, s, :]))
                        v.wait()
                        dve.sem_inc(var2_ready, 1)

                    def take_scales(c, i):
                        dve.wait_ge(std2_ready, c + 1)
                        v(nc.vector.reciprocal(rstd[i % 2][:, :], std[i % 2][:, :]))
                        v.wait()
                        v(nc.vector.scalar_tensor_tensor(shift[i % 2][:, :], moments[i % 2][:, :, 0], -1.0, rstd[i % 2][:, :], ALU.mult, ALU.mult))
                        v.wait()
                        dve.sem_inc(scales_ready, 1)

                    def chunks(q, first):
                        for i in range(YB):
                            take_moments(q * YB + i, i, first)
                            if not (first and i == 0):
                                take_scales(q * YB + i - 1, (i - 1) % YB)
                        v.restart()
                    chunks(0, True)
                    if NQ > 1:
                        with dve.Fori(1, NQ) as q:
                            chunks(q, False)
                    take_scales(NC - 1, YB - 1)


def kernel(x, adj, L1_gnn_w_self_0, L1_gnn_w_neigh_0, L1_gnn_w_self_1, L1_gnn_w_neigh_1):
    import numpy as _np
    import concourse.bacc as _bacc
    from concourse.bass_utils import run_bass_kernel_spmd as _run

    given = {
        "x": x, "adj": adj, "w_self_0": L1_gnn_w_self_0, "w_neigh_0": L1_gnn_w_neigh_0,
        "w_self_1": L1_gnn_w_self_1, "w_neigh_1": L1_gnn_w_neigh_1,
    }
    nc = _bacc.Bacc("TRN2", target_bir_lowering=False, num_devices=1)
    arrays, args = {}, []
    for name, a in given.items():
        a = _np.ascontiguousarray(a)
        arrays[f"in_{name}"] = a
        args.append(nc.dram_tensor(f"in_{name}", a.shape, mybir.dt.from_np(a.dtype), kind="ExternalInput").ap())
    out = nc.dram_tensor("out_0", arrays["in_x"].shape, mybir.dt.float32, kind="ExternalOutput").ap()
    graph_max_then_sum_layers(nc, *args, out)
    r = _run(nc, [arrays], core_ids=[0])
    return r.results[0]["out_0"]
```
